# Optimizing a Trainium2 kernel written in Bass

```python
import numpy as np
import jax
import jax.numpy as jnp

def _softmax(x, axis=-1):
    return jax.nn.softmax(x, axis=axis)

def _gelu(x):
    return jax.nn.gelu(x, approximate=True)

def _silu(x):
    return jax.nn.silu(x)

def _sigmoid(x):
    return jax.nn.sigmoid(x)

def _layernorm(x, axis=-1, eps=1e-05):
    m = jnp.mean(x, axis=axis, keepdims=True)
    v = jnp.var(x, axis=axis, keepdims=True)
    return (x - m) / jnp.sqrt(v + eps)

def _scatter_add(tgt, idx, src, axis=0):
    return tgt.at[idx].add(src)

def _segment_sum(src, seg, n):
    return jax.ops.segment_sum(src, seg, n)
kernel_name = 'mk_decoder_preln_d1_seqx_r8_393b5d'

def setup_inputs(seed: int=0):
    np.random.seed(seed)
    _w = jnp.asarray

    def _rec_inputs():
        import jax
        import jax.numpy as jnp
        _rk = jax.random.key(seed)
        x = -0.0002928 + 1 * jax.random.normal(jax.random.fold_in(_rk, 1), (16, 128, 256), jnp.float32)
        _lenS = 128 - jax.random.randint(jax.random.fold_in(_rk, 7), (16,), 0, max(1, 128 // 4) + 1, jnp.int32)
        _lenS2 = 128 - jax.random.randint(jax.random.fold_in(_rk, 8), (16,), 0, max(1, 128 // 4) + 1, jnp.int32)
        _ctx_512P = jax.random.normal(jax.random.fold_in(_rk, 11), (16, 16, 64), jnp.float32)
        _ctx_512c = jax.random.dirichlet(jax.random.fold_in(_rk, 511), 0.3 * jnp.ones((16,), jnp.float32), (16, 128))
        _ctx_512t = jnp.einsum('bsk,bkd->bsd', _ctx_512c, _ctx_512P)
        _ctx_512t = _ctx_512t * jax.lax.rsqrt(jnp.mean(jnp.square(_ctx_512t)) + 1e-12) * 0.953939
        ctx_512 = 0.000227908 + 0.99994 * (_ctx_512t + 0.3 * jax.random.normal(jax.random.fold_in(_rk, 611), (16, 128, 64), jnp.float32))
        return (x, ctx_512)
    x, ctx_512 = _rec_inputs()

    def _L0_attn_setup():
        import jax, jax.numpy as jnp
        import numpy as np
        D_MODEL = 256
        N_HEADS = 16
        N_KV = 4
        HEAD_DIM = 128
        SUB = 64
        WINDOW = 64
        THETA = 10000.0
        NEG = jnp.float32(-1e+30)

        def _rope_tables(seq_len):
            inv_freq = 1.0 / THETA ** (jnp.arange(0, HEAD_DIM, 2, dtype=jnp.float32) / HEAD_DIM)
            freqs = jnp.arange(seq_len, dtype=jnp.float32)[:, None] * inv_freq[None, :]
            emb = jnp.concatenate([freqs, freqs], axis=-1)
            return (jnp.cos(emb), jnp.sin(emb))

        def _rotate_half(x):
            x1, x2 = (x[..., :HEAD_DIM // 2], x[..., HEAD_DIM // 2:])
            return jnp.concatenate([-x2, x1], axis=-1)

        def _apply_rope(t, cos, sin):
            c = cos[None, None]
            s = sin[None, None]
            return t * c + _rotate_half(t) * s
        key = jax.random.key(seed)
        ks = jax.random.split(key, 6)
        B, S = (1, 256)
        std = 0.02
        return {'x': jax.random.normal(ks[0], (B, S, D_MODEL), dtype=jnp.float32), 'Wq': jax.random.normal(ks[1], (D_MODEL, N_HEADS * HEAD_DIM), dtype=jnp.float32) * std, 'Wk': jax.random.normal(ks[2], (D_MODEL, N_KV * HEAD_DIM), dtype=jnp.float32) * std, 'Wv': jax.random.normal(ks[3], (D_MODEL, N_KV * HEAD_DIM), dtype=jnp.float32) * std, 'Wo': jax.random.normal(ks[4], (N_HEADS * HEAD_DIM, D_MODEL), dtype=jnp.float32) * std, 'lam': jnp.full((N_HEADS,), 0.1, dtype=jnp.float32)}
    _L0_attn_all = _L0_attn_setup()
    _L0_attn_in = {k: v for k, v in _L0_attn_all.items() if k in ('Wq', 'Wk', 'Wv', 'Wo', 'lam')}
    del _L0_attn_all

    def _L0_xattn_setup():
        import jax, jax.numpy as jnp
        import numpy as np
        B, S, L = (2, 128, 128)
        DIM_Q, H, K, D_C, D_CQ, R = (256, 16, 128, 64, 192, 64)

        def _rope_tables(length, dim):
            inv = 1.0 / 10000.0 ** (jnp.arange(0, dim, 2, dtype=jnp.float32) / dim)
            f = jnp.arange(length, dtype=jnp.float32)[:, None] * inv[None, :]
            sin = jnp.repeat(jnp.sin(f), 2, axis=-1)
            cos = jnp.repeat(jnp.cos(f), 2, axis=-1)
            return (sin, cos)

        def _rotate_half(x):
            half = x.shape[-1] // 2
            return jnp.concatenate([-x[..., half:], x[..., :half]], axis=-1)

        def _apply_rope(x, sin, cos):
            return x * cos + _rotate_half(x) * sin
        key = jax.random.key(seed)
        ks = jax.random.split(key, 8)
        return {'hidden_q': jax.random.normal(ks[0], (B, S, DIM_Q), jnp.float32), 'kv_c': jax.random.normal(ks[1], (B, L, D_C), jnp.float32), 'Wq': jax.random.normal(ks[2], (H * K, DIM_Q), jnp.float32) / np.sqrt(DIM_Q).astype(np.float32), 'w_kc_q': jax.random.normal(ks[3], (H, K, D_CQ), jnp.float32) / np.sqrt(K).astype(np.float32), 'w_kc_kv': jax.random.normal(ks[4], (H, K, D_C), jnp.float32) / np.sqrt(K).astype(np.float32), 'W_qr': jax.random.normal(ks[5], (H, D_CQ, R), jnp.float32) / np.float32(np.sqrt(D_CQ) * np.sqrt(R)), 'W_kr': jax.random.normal(ks[6], (H, D_C, R), jnp.float32) / np.sqrt(D_C).astype(np.float32), 'Wo': jax.random.normal(ks[7], (DIM_Q, H * K), jnp.float32) / np.sqrt(H * K).astype(np.float32)}
    _L0_xattn_all = _L0_xattn_setup()
    _L0_xattn_in = {k: v for k, v in _L0_xattn_all.items() if k in ('Wq', 'w_kc_q', 'w_kc_kv', 'W_qr', 'W_kr', 'Wo')}
    del _L0_xattn_all

    def _L0_ffn_setup():
        import jax, jax.numpy as jnp
        import numpy as np
        H, I, E, TOP_K = (256, 176, 16, 6)
        IS = 352
        NORM_TOPK_PROB = False

        def _silu_and_mul(gate_up):
            d = gate_up.shape[-1] // 2
            g, u = (gate_up[..., :d], gate_up[..., d:])
            return jax.nn.silu(g) * u
        key = jax.random.key(seed)
        ks = jax.random.split(key, 6)
        s = 0.02
        return {'x': jax.random.normal(ks[0], (1, 256, H), jnp.float32), 'gate_w': jax.random.normal(ks[1], (E, H), jnp.float32) * s, 'w1': jax.random.normal(ks[2], (E, 2 * I, H), jnp.float32) * s, 'w2': jax.random.normal(ks[3], (E, H, I), jnp.float32) * s, 'shared_w1': jax.random.normal(ks[4], (2 * IS, H), jnp.float32) * s, 'shared_w2': jax.random.normal(ks[5], (H, IS), jnp.float32) * s}
    _L0_ffn_all = _L0_ffn_setup()
    _L0_ffn_in = {k: v for k, v in _L0_ffn_all.items() if k in ('gate_w', 'w1', 'w2', 'shared_w1', 'shared_w2')}
    del _L0_ffn_all
    return {'x': x, 'ctx_512': ctx_512, 'L0_attn_Wq': _L0_attn_in['Wq'], 'L0_attn_Wk': _L0_attn_in['Wk'], 'L0_attn_Wv': _L0_attn_in['Wv'], 'L0_attn_Wo': _L0_attn_in['Wo'], 'L0_attn_lam': _L0_attn_in['lam'], 'L0_xattn_Wq': _L0_xattn_in['Wq'], 'L0_xattn_w_kc_q': _L0_xattn_in['w_kc_q'], 'L0_xattn_w_kc_kv': _L0_xattn_in['w_kc_kv'], 'L0_xattn_W_qr': _L0_xattn_in['W_qr'], 'L0_xattn_W_kr': _L0_xattn_in['W_kr'], 'L0_xattn_Wo': _L0_xattn_in['Wo'], 'L0_ffn_gate_w': _L0_ffn_in['gate_w'], 'L0_ffn_w1': _L0_ffn_in['w1'], 'L0_ffn_w2': _L0_ffn_in['w2'], 'L0_ffn_shared_w1': _L0_ffn_in['shared_w1'], 'L0_ffn_shared_w2': _L0_ffn_in['shared_w2']}

def reference(x, ctx_512, L0_attn_Wq, L0_attn_Wk, L0_attn_Wv, L0_attn_Wo, L0_attn_lam, L0_xattn_Wq, L0_xattn_w_kc_q, L0_xattn_w_kc_kv, L0_xattn_W_qr, L0_xattn_W_kr, L0_xattn_Wo, L0_ffn_gate_w, L0_ffn_w1, L0_ffn_w2, L0_ffn_shared_w1, L0_ffn_shared_w2):
    import jax
    import jax.numpy as jnp

    def _L0_attn_ref(x, Wq, Wk, Wv, Wo, lam):
        import jax, jax.numpy as jnp
        import numpy as np
        D_MODEL = 256
        N_HEADS = 16
        N_KV = 4
        HEAD_DIM = 128
        SUB = 64
        WINDOW = 64
        THETA = 10000.0
        NEG = jnp.float32(-1e+30)

        def _rope_tables(seq_len):
            inv_freq = 1.0 / THETA ** (jnp.arange(0, HEAD_DIM, 2, dtype=jnp.float32) / HEAD_DIM)
            freqs = jnp.arange(seq_len, dtype=jnp.float32)[:, None] * inv_freq[None, :]
            emb = jnp.concatenate([freqs, freqs], axis=-1)
            return (jnp.cos(emb), jnp.sin(emb))

        def _rotate_half(x):
            x1, x2 = (x[..., :HEAD_DIM // 2], x[..., HEAD_DIM // 2:])
            return jnp.concatenate([-x2, x1], axis=-1)

        def _apply_rope(t, cos, sin):
            c = cos[None, None]
            s = sin[None, None]
            return t * c + _rotate_half(t) * s
        B, S, _ = x.shape
        n_rep = N_HEADS // N_KV
        q = (x @ Wq).reshape(B, S, N_HEADS, HEAD_DIM).transpose(0, 2, 1, 3)
        k = (x @ Wk).reshape(B, S, N_KV, HEAD_DIM).transpose(0, 2, 1, 3)
        v = (x @ Wv).reshape(B, S, N_KV, HEAD_DIM).transpose(0, 2, 1, 3)
        cos, sin = _rope_tables(S)
        q = _apply_rope(q, cos, sin)
        k = _apply_rope(k, cos, sin)
        k = jnp.repeat(k, n_rep, axis=1)
        v = jnp.repeat(v, n_rep, axis=1)
        q1, q2 = (q[..., :SUB], q[..., SUB:])
        k1, k2 = (k[..., :SUB], k[..., SUB:])
        scale = 1.0 / jnp.sqrt(jnp.float32(SUB))
        s1 = jnp.einsum('bhqd,bhkd->bhqk', q1, k1) * scale
        s2 = jnp.einsum('bhqd,bhkd->bhqk', q2, k2) * scale
        i = jnp.arange(S)[:, None]
        j = jnp.arange(S)[None, :]
        allowed = (j <= i) & (j >= i - WINDOW + 1)
        s1 = jnp.where(allowed[None, None], s1, NEG)
        s2 = jnp.where(allowed[None, None], s2, NEG)
        a1 = jax.nn.softmax(s1.astype(jnp.float32), axis=-1).astype(x.dtype)
        a2 = jax.nn.softmax(s2.astype(jnp.float32), axis=-1).astype(x.dtype)
        diff = jax.nn.relu(a1 - lam[None, :, None, None] * a2)
        diff = diff / (jnp.sum(diff, axis=-1, keepdims=True) + 1e-06)
        out = jnp.einsum('bhqk,bhkd->bhqd', diff, v)
        out = out.transpose(0, 2, 1, 3).reshape(B, S, N_HEADS * HEAD_DIM)
        return out @ Wo

    def _L0_xattn_ref(hidden_q, kv_c, Wq, w_kc_q, w_kc_kv, W_qr, W_kr, Wo):
        import jax, jax.numpy as jnp
        import numpy as np
        B, S, L = (2, 128, 128)
        DIM_Q, H, K, D_C, D_CQ, R = (256, 16, 128, 64, 192, 64)

        def _rope_tables(length, dim):
            inv = 1.0 / 10000.0 ** (jnp.arange(0, dim, 2, dtype=jnp.float32) / dim)
            f = jnp.arange(length, dtype=jnp.float32)[:, None] * inv[None, :]
            sin = jnp.repeat(jnp.sin(f), 2, axis=-1)
            cos = jnp.repeat(jnp.cos(f), 2, axis=-1)
            return (sin, cos)

        def _rotate_half(x):
            half = x.shape[-1] // 2
            return jnp.concatenate([-x[..., half:], x[..., :half]], axis=-1)

        def _apply_rope(x, sin, cos):
            return x * cos + _rotate_half(x) * sin
        Bv, Sv, _ = hidden_q.shape
        _, Lv, _ = kv_c.shape
        q_hk = (hidden_q @ Wq.T).reshape(Bv, Sv, H, K)
        q_big = jnp.einsum('bshk,hkq->bshq', q_hk, w_kc_q)
        sin_q, cos_q = _rope_tables(Sv, D_CQ)
        q_big = _apply_rope(q_big, sin_q[None, :, None, :], cos_q[None, :, None, :])
        sin_k, cos_k = _rope_tables(Lv, D_C)
        kv_r = _apply_rope(kv_c, sin_k[None], cos_k[None])
        q_r = jnp.einsum('bshq,hqr->bhsr', q_big, W_qr)
        k_r = jnp.einsum('bld,hdr->bhlr', kv_r, W_kr)
        scores = jnp.einsum('bhsr,bhlr->bhsl', q_r, k_r)
        attn = jax.nn.softmax(scores, axis=-1)
        ctx_c = jnp.einsum('bhsl,bld->bhsd', attn, kv_r)
        ctx_lat = jnp.einsum('bhsd,hkd->bhsk', ctx_c, w_kc_kv)
        ctx = ctx_lat.transpose(0, 2, 1, 3).reshape(Bv, Sv, H * K)
        return ctx @ Wo.T

    def _L0_ffn_ref(x, gate_w, w1, w2, shared_w1, shared_w2):
        import jax, jax.numpy as jnp
        import numpy as np
        H, I, E, TOP_K = (256, 176, 16, 6)
        IS = 352
        NORM_TOPK_PROB = False

        def _silu_and_mul(gate_up):
            d = gate_up.shape[-1] // 2
            g, u = (gate_up[..., :d], gate_up[..., d:])
            return jax.nn.silu(g) * u
        B, S, Hd = x.shape
        xf = x.reshape(-1, Hd)
        T = xf.shape[0]
        shared_out = _silu_and_mul(xf @ shared_w1.T) @ shared_w2.T
        logits = xf @ gate_w.T
        probs = jax.nn.softmax(logits.astype(jnp.float32), axis=-1)
        routing_weights, selected = jax.lax.top_k(probs, TOP_K)
        if NORM_TOPK_PROB:
            routing_weights = routing_weights / routing_weights.sum(-1, keepdims=True)
        combine = jnp.zeros((T, E), jnp.float32).at[jnp.arange(T)[:, None], selected].add(routing_weights).astype(x.dtype)
        gate_up = jnp.einsum('th,eoh->teo', xf, w1)
        act = _silu_and_mul(gate_up)
        moe_out = jnp.einsum('te,tei,ehi->th', combine, act, w2)
        return (moe_out + shared_out).reshape(B, S, Hd)
    x = x + _L0_attn_ref(_layernorm(x, axis=-1), L0_attn_Wq, L0_attn_Wk, L0_attn_Wv, L0_attn_Wo, L0_attn_lam)
    x = x + _L0_xattn_ref(_layernorm(x, axis=-1), ctx_512, L0_xattn_Wq, L0_xattn_w_kc_q, L0_xattn_w_kc_kv, L0_xattn_W_qr, L0_xattn_W_kr, L0_xattn_Wo)
    x = x + _L0_ffn_ref(_layernorm(x, axis=-1), L0_ffn_gate_w, L0_ffn_w1, L0_ffn_w2, L0_ffn_shared_w1, L0_ffn_shared_w2)
    return x

_drawn_inputs = setup_inputs


def setup_inputs(seed=0):
    import zlib

    import numpy as np

    out = dict(_drawn_inputs(seed))
    spreads = {'L0_attn_lam': (0.10000000149011612, 0.6)}
    factors = {'L0_attn_Wq': 8.0,
     'L0_attn_Wk': 8.0,
     'L0_ffn_gate_w': 8.0,
     'L0_ffn_w1': 8.0,
     'L0_ffn_w2': 8.0,
     'L0_ffn_shared_w1': 2.969,
     'L0_ffn_shared_w2': 2.977}
    for name, (base, spread) in spreads.items():
        noise = np.random.default_rng([zlib.crc32(name.encode()), seed]).standard_normal(out[name].shape)
        drawn = base * np.exp(spread * noise) if base else spread * noise
        out[name] = jnp.asarray(drawn.astype(out[name].dtype))
    for name, factor in factors.items():
        out[name] = (out[name] * factor).astype(out[name].dtype)
    return out
```

```python
import concourse.bass as bass
from concourse import mybir
from contextlib import ExitStack

B, S, DM = 16, 128, 256
KT = DM // 128
CB = 4
NC = B // CB
CW = CB * S
H, HG = 16, 4
NG = H // HG
UN = B
WINDOW = 64
LN_EPS = 1e-5
DIFF_EPS = 1e-6
NEG = -1e30
XQ, XC = 192, 64
XT = HG * XQ // 128
XP = HG // 2
E, EI, SI, TOPK = 16, 176, 352, 6
IT = (E * EI + 384) // 128
TG = 5
CG = IT // TG
KC = 64

RB_WQ, RB_KCQ = 0, HG * DM
RB_QR = RB_KCQ + HG * XQ
RB_KR = RB_QR + XP * 2 * 2 * XQ
RB_KV = RB_KR + XP * 128
RB_WO = RB_KV + HG * XC
RB_N = RB_WO + HG * DM

GATE_STEPS = 20

RC_T = 2 * KT * 128 + DM
RC_N = TG * RC_T + TG * 128


def wait(eng, sem, value):
    if isinstance(value, int) and value <= 0:
        return
    eng.wait_ge(sem, value)


def decoder_kernel(nc, x, ctx_in, in_wqk, in_wv, in_wo, in_lam, in_taba, in_rawb, in_tabb, in_kvtab,
                   in_rawc, in_gate, ident, mask, out):
    f32, f32r, bf16 = mybir.dt.float32, mybir.dt.float32r, mybir.dt.bfloat16
    ALU, ACT, AX = mybir.AluOpType, mybir.ActivationFunctionType, mybir.AxisListType
    ctx = ExitStack()

    def sem(name):
        return ctx.enter_context(nc.semaphore(name))

    def sb(stack, name, shape, dt=f32):
        return stack.enter_context(nc.sbuf_tensor(name, shape, dt))

    with ctx:
        x_sb = sb(ctx, "x_sb", [128, B, DM])
        xnf = sb(ctx, "xnf", [128, KT, B * S])
        xnh = sb(ctx, "xnh", [128, KT, B * S], f32r)
        xnl = sb(ctx, "xnl", [128, KT, B * S], f32r)
        xnt = sb(ctx, "xnt", [128, 2, CB, DM])
        stats = sb(ctx, "stats", [128, B, 6])
        mv = sb(ctx, "mv", [128, B, 2])
        veps = sb(ctx, "veps", [128, B])
        rstd = sb(ctx, "rstd", [128, B])
        mhalf = sb(ctx, "mhalf", [128, B])
        idf = sb(ctx, "idf", [128, 128])
        idb = sb(ctx, "idb", [128, 128], bf16)
        maskf = sb(ctx, "maskf", [128, 128])
        maskb = sb(ctx, "maskb", [128, 128], bf16)
        raw_b = sb(ctx, "raw_b", [128, RB_N])
        negmax = sb(ctx, "negmax", [128, 2, 8])
        sums = sb(ctx, "sums", [128, 2, 8])
        rec2 = sb(ctx, "rec2", [128, 2, 4])
        ratio = sb(ctx, "ratio", [128, 2, 4])
        rho = sb(ctx, "rho", [128, 2, 4])
        rsum = sb(ctx, "rsum", [128, 2, 4])
        den = sb(ctx, "den", [128, 2, 4])
        rden = sb(ctx, "rden", [128, 2, 4])
        dnorm = sb(ctx, "dnorm", [128, 2, HG, S])
        pt = sb(ctx, "pt", [128, 2, HG, S])

        am = ExitStack()
        raw_a = sb(am, "raw_a", [128, KT, 768])
        wah = sb(am, "wah", [128, KT, 768], f32r)
        wal = sb(am, "wal", [128, KT, 768], f32r)
        wv = sb(am, "wv", [128, KT, (NG + 1) * 128])
        wo = sb(am, "wo", [128, H, DM])
        nlam = sb(am, "nlam", [128, H])
        taba = sb(am, "taba", [128, 6, S])
        qa = sb(am, "qa", [128, 2, HG, CW])
        qb = sb(am, "qb", [128, 2, HG, CW])
        ktmp = sb(am, "ktmp", [128, 2, CW])
        k1 = sb(am, "k1", [128, 2, CW])
        k2 = sb(am, "k2", [128, 2, CW])
        va = sb(am, "va", [128, 2, CB, 128])
        ea = sb(am, "ea", [128, 2, 2, HG, S])
        oa = sb(am, "oa", [128, 2, HG, S])
        am.close()
        bm = ExitStack()
        wbh = sb(bm, "wbh", [128, XT, KT, 128], f32r)
        wbl = sb(bm, "wbl", [128, XT, KT, 128], f32r)
        mq = sb(bm, "mq", [128, XT, 2, 128])
        wco = sb(bm, "wco", [128, XP, DM])
        tabb = sb(bm, "tabb", [128, 3, 2, S])
        qcs = sb(bm, "qcs", [128, XT, 2, CW])
        qr = sb(bm, "qr", [128, 2, XP, CW])
        kvtab = sb(bm, "kvtab", [128, 2, XC])
        kvin = sb(bm, "kvin", [128, B, XC])
        kvt = sb(bm, "kvt", [128, B, XC])
        kvr = sb(bm, "kvr", [128, B, 2, XC])
        kbd = sb(bm, "kbd", [128, B, 2, S])
        eb = sb(bm, "eb", [128, 2, HG, S])
        ob = sb(bm, "ob", [128, 2, XP, S])
        bm.close()
        cm = ExitStack()
        raw_c = sb(cm, "raw_c", [128, RC_N])
        wch = sb(cm, "wch", [128, TG, RC_T], f32r)
        wcl = sb(cm, "wcl", [128, TG, RC_T], f32r)
        sel = sb(cm, "sel", [KC, TG, 128], bf16)
        gw = sb(cm, "gw", [128, KT, E])
        combt = sb(cm, "combt", [KC, B * S], bf16)
        cmb = sb(cm, "cmb", [128, B, KC], bf16)
        sg = sb(cm, "sg", [128, 2, CW])
        hu = sb(cm, "hu", [128, 2, CW])
        hh = sb(cm, "hh", [128, 2, CW])
        hhh = sb(cm, "hhh", [128, 2, CW], f32r)
        hhl = sb(cm, "hhl", [128, 2, CW], f32r)
        gl = sb(cm, "gl", [128, B, E])
        ge = sb(cm, "ge", [128, B, E])
        gp = sb(cm, "gp", [128, B, E])
        g8 = sb(cm, "g8", [128, B, 8])
        ggt = sb(cm, "ggt", [128, B, E])
        geq = sb(cm, "geq", [128, B, E])
        gcum = sb(cm, "gcum", [128, B, E])
        gone = sb(cm, "gone", [128, B, E])
        gr1 = sb(cm, "gr1", [128, B, E])
        gr2 = sb(cm, "gr2", [128, B, E])
        gmx = sb(cm, "gmx", [128, B])
        gsum = sb(cm, "gsum", [128, B])
        grec = sb(cm, "grec", [128, B])
        gn = sb(cm, "gn", [128, B])
        glim = sb(cm, "glim", [128, B])
        cm.close()

        ps = ctx.enter_context(nc.psum_tensor("ps", [128, 8, 512], f32))

        def bank(n):
            return ps[:, n, :]

        def quads(ap):
            return ap.rearrange("p (h k) -> p h k", k=S)

        s_x = [sem(f"x_loaded{c}") for c in range(NC)]
        s_const, s_cst = sem("const_loaded"), sem("const_ready")
        ln_st, ln_ag, ln_var = sem("ln_stats"), sem("ln_aggr"), sem("ln_var")
        ln_rs, ln_xt = sem("ln_rstd"), sem("ln_token_major")
        ln_tp, ln_f = sem("ln_transposed"), sem("ln_feature_major")
        ln_h, ln_l = sem("ln_high"), sem("ln_low")
        a_raw, a_wld = sem("a_raw_loaded"), sem("a_weights_loaded")
        a_hi, a_lo = sem("a_w_high"), sem("a_w_low")
        a_pj, a_pf, a_k = sem("a_projected"), sem("a_projection_taken"), sem("a_k_ready")
        a_sc, a_mx, a_ex = sem("a_scores"), sem("a_negmax"), sem("a_exp")
        a_r2, a_rt, a_rh = sem("a_rec2"), sem("a_ratio"), sem("a_rho")
        a_df, a_re, a_dd = sem("a_difference"), sem("a_clipped"), sem("a_denominator")
        a_cb, a_dn = sem("a_norm_ready"), sem("a_weights_normed")
        a_tp, a_pt, a_pv = sem("a_transposed"), sem("a_pt_ready"), sem("a_pv")
        a_o, a_wo, a_y, a_nl = sem("a_o_ready"), sem("a_out"), sem("a_x_added"), sem("a_nlam_ready")
        b_raw_s, b_ctx = sem("b_raw_loaded"), sem("b_ctx_loaded")
        b_kv, b_kz = sem("b_kv_step"), sem("b_kv_zeroed")
        b_kvp, b_kvc = sem("b_kv_transposed"), sem("b_kv_block")
        b_it, b_if, b_m = sem("b_item_done"), sem("b_item_taken"), sem("b_high_and_m_ready")
        b_qr, b_qs = sem("b_qr"), sem("b_qr_ready")
        b_sc, b_mx, b_ex = sem("b_scores"), sem("b_negmax"), sem("b_exp")
        b_rs, b_dn = sem("b_rsum"), sem("b_weights_normed")
        b_tp, b_pt, b_pv = sem("b_transposed"), sem("b_pt_ready"), sem("b_pv")
        b_o, b_wo, b_y = sem("b_o_ready"), sem("b_out"), sem("b_x_added")
        c_raw_s = sem("c_raw_loaded")
        c_hi, c_lo = sem("c_w_high"), sem("c_w_low")
        c_lg, c_gs, c_ge = sem("c_logits"), sem("c_gate_step"), sem("c_gate_exp")
        c_ct, c_cc = sem("c_comb_transposed"), sem("c_comb_ready")
        c_g, c_u, c_c = sem("c_gate_done"), sem("c_up_done"), sem("c_comb_spread")
        c_sg, c_hu, c_h = sem("c_silu"), sem("c_silu_up"), sem("c_hidden_ready")
        c_hr, c_l = sem("c_hidden_high"), sem("c_hidden_low")
        c_dn, c_y = sem("c_down_done"), sem("c_x_added")
        s_out, s_cst2, c_gws = sem("out_stored"), sem("mhalf_ready"), sem("c_gate_weights_loaded")
        block = ctx.enter_context(nc.Block())

        A_ITEMS = ["k", "k'", "q0", "q1", "q2", "q3", "v"]
        AN, AV = len(A_ITEMS), A_ITEMS.index("v")
        A_SLOT = {(0, 0): 0, (0, 1): 1, (1, 0): 2, (1, 1): 3, (2, 0): 4, (2, 1): 5, (3, 0): 6}
        AW = AN - 1

        def bcast(tab):
            return tab.unsqueeze(1).broadcast_to([128, CB, S])

        B_STEP = [("qb", 0), ("qb", 1), ("qb", 2), ("qb", 3), ("qr", 0), ("qb", 4), ("qb", 5), ("qr", 1)]
        B_PREP = {(10, 1): 0, (11, 0): 1, (11, 1): 2, (12, 0): 3, (12, 1): 4, (13, 0): 5}

        def b_slot(u, s):
            if s == 2:
                return [("wco", 0), ("wco", 1)] if u == 2 else []
            return [B_STEP[2 * (u % CB) + s]] + ([("prep", B_PREP[u, s])] if (u, s) in B_PREP else [])

        B_PLACE = {}
        for u_ in range(UN):
            for s_ in range(3):
                for what_ in b_slot(u_, s_):
                    if what_[0] != "qr":
                        B_PLACE[u_, s_, what_] = len(B_PLACE)
        BN = len(B_PLACE)
        B_FIRST = [("prep", t) for t in range(XT)] + B_STEP
        BF = 2 * XT
        assert BN % 2 == 0 and BF % 2 == 0

        def b_item(g, u, s, what):
            return g * BN + (BF + B_PLACE[u, s, what])

        def b_last(g, u, s, kind, t):
            ahead = [B_PLACE[k] for k in B_PLACE if k[2] == (kind, t) and (k[0], k[1]) <= (u, s)]
            if ahead:
                return g * BN + (BF + max(ahead))
            return (g - 1) * BN + (BF + max(B_PLACE[k] for k in B_PLACE if k[2] == (kind, t)))

        A_S, B_S = [ps[:, 0:2, :], ps[:, 2:4, :]], [ps[:, 0, :], ps[:, 1, :]]
        PTB, OB, YB, PJ, QRB = 4, 5, 6, 7, 7
        C_G, C_U, C_C = [2, 3], [4, 5], [6, 7]

        def a_over(eng):
            eng.wait_ge(a_y, NG * UN)
            eng.wait_ge(a_pf, (NG * NC + 1) * AN)
            eng.wait_ge(a_k, NG * NC + 1)
            eng.wait_ge(a_lo, AW * (NG + 1))
            eng.wait_ge(a_raw, 16 * (NG + 1))

        def b_over(eng):
            eng.wait_ge(b_y, NG * UN)
            eng.wait_ge(b_if, BF + NG * BN)
            eng.wait_ge(b_qs, XP * (NG * NC + 1))

        @block.sync
        def _(sp):
            for c in range(NC):
                sp.dma_start(x_sb[:, CB * c:CB * (c + 1), :],
                             x[CB * c:CB * (c + 1)].rearrange("b p d -> p b d")).then_inc(s_x[c], 16)
                if c == 0:
                    sp.dma_start(idf[:, :], ident).then_inc(s_const, 16)
                    sp.dma_start(maskf[:, :], mask).then_inc(s_const, 16)
                    sp.dma_start(raw_a[:, :, :], in_wqk[0]).then_inc(a_raw, 16)
            sp.dma_start(taba[:, :, :], in_taba).then_inc(a_wld, 16)
            sp.dma_start(wv[:, :, :], in_wv).then_inc(a_wld, 16)
            sp.dma_start(nlam[:, :], in_lam).then_inc(a_wld, 16)
            sp.dma_start(wo[:, :, :], in_wo).then_inc(a_wld, 16)
            sp.dma_start(raw_b[:, :], in_rawb[0]).then_inc(b_raw_s, 16)
            with sp.Fori(0, NG) as g:
                sp.wait_ge(a_lo, g * AW + AW)
                sp.dma_start(raw_a[:, :, :], in_wqk[bass.ds(g + 1, 1)].rearrange("o p k n -> p (o k) n"))\
                  .then_inc(a_raw, 16)
            a_over(sp)
            sp.dma_start(kvin[:, :, :], ctx_in.rearrange("b p d -> p b d")).then_inc(b_ctx, 16)
            sp.dma_start(kvtab[:, :, :], in_kvtab).then_inc(b_ctx, 16)
            sp.dma_start(tabb[:, :, :, :], in_tabb).then_inc(b_ctx, 16)
            with sp.Fori(0, NG) as g:
                sp.wait_ge(b_if, g * BN + (BF + B_PLACE[2, 2, ("wco", 1)] + 1))
                sp.dma_start(raw_b[:, :], in_rawb[bass.ds(g + 1, 1)].rearrange("o p n -> p (o n)"))\
                  .then_inc(b_raw_s, 16)
            b_over(sp)
            sp.dma_start(raw_c[:, :], in_rawc[0]).then_inc(c_raw_s, 16)
            sp.dma_start(gw[:, :, :], in_gate).then_inc(c_gws, 16)
            with sp.Fori(0, CG) as g:
                sp.wait_ge(c_lo, g * TG + TG)
                sp.dma_start(raw_c[:, :], in_rawc[bass.ds(g + 1, 1)].rearrange("o p n -> p (o n)"))\
                  .then_inc(c_raw_s, 16)
            for c in range(NC):
                sp.wait_ge(c_y, (CG - 1) * NC + c + 1)
                sp.dma_start(out[CB * c:CB * (c + 1)].rearrange("b p d -> p b d"),
                             x_sb[:, CB * c:CB * (c + 1), :]).then_inc(s_out, 16)
            sp.wait_ge(c_raw_s, 16 * (CG + 1))
            sp.wait_ge(s_out, 16 * NC)

        @block.tensor
        def _(pe):
            def three_pass(out_ap, wh, wl, c):
                tok = slice(CW * c, CW * (c + 1))
                steps = [(w(kt), m[:, kt, tok]) for kt in range(KT) for w, m in ((wh, xnh), (wh, xnl), (wl, xnh))]
                for n, (w, m) in enumerate(steps):
                    last = pe.matmul(out_ap, w, m, start=n == 0, stop=n == len(steps) - 1)
                return last

            def layer_norm(stage):
                for c in range(NC):
                    m = stage * NC + c
                    pe.wait_ge(ln_xt, m + 1)
                    for kt in range(KT):
                        if c >= 2:
                            pe.wait_ge(ln_f, 2 * (m - 2) + kt + 1)
                        for j in range(CB):
                            last = pe.transpose(quads(bank(2 * (c % 2) + kt))[:, j, :],
                                                xnt[:, c % 2, j, 128 * kt:128 * (kt + 1)], idf[:, :])
                        last.then_inc(ln_tp, 1)

            def a_project(g_to, c, item, fresh):
                n = (g_to * NC + c) * AN + item
                wait(pe, a_pf, n)
                if item == AV:
                    for j in range(CB):
                        tok = slice(S * (CB * c + j), S * (CB * c + j + 1))
                        for kt in range(KT):
                            last = pe.matmul(quads(bank(PJ))[:, j, :], xnf[:, kt, tok],
                                             wv[:, kt, bass.ds(g_to * 128, 128)], start=kt == 0, stop=kt == KT - 1)
                else:
                    if fresh:
                        pe.wait_ge(a_lo, g_to * AW + (item + 1))
                    t = slice(128 * item, 128 * item + 128)
                    last = three_pass(bank(PJ), lambda kt: wah[:, kt, t], lambda kt: wal[:, kt, t], c)
                last.then_inc(a_pj, 1)

            def a_unit(g, u, first=False, drain=False):
                n, c, j = g * UN + u, u // CB, u % CB

                def slot(s):
                    if not drain and (j, s) in A_SLOT:
                        ahead = c == NC - 1
                        a_project(g + 1 if ahead else g, (c + 1) % NC, A_SLOT[j, s], ahead)
                slot(0)
                if not drain:
                    if j == 0:
                        pe.wait_ge(a_pf, (g * NC + (c + 1)) * AN)
                        pe.wait_ge(a_k, g * NC + (c + 1))
                    wait(pe, a_ex, n - 1)
                    tok = slice(S * j, S * (j + 1))
                    for m, (q_, k_) in enumerate(((qa, k1), (qb, k2))):
                        sc = quads(A_S[u % 2][:, m, :])
                        pe.matmul(sc, idb[:, :], maskb[:, :].unsqueeze(1).broadcast_to([128, HG, S]),
                                  start=True, stop=False, skip_group_check=True)
                        for h in range(HG):
                            last = pe.matmul(sc[:, h, :], q_[:, c % 2, h, tok], k_[:, c % 2, tok],
                                             start=False, stop=h == HG - 1, skip_group_check=True)
                    last.then_inc(a_sc, 1)
                two = not (first and u < 2) and not (drain and u >= 2)
                if two:
                    pe.wait_ge(a_dn, n - 1)
                    wait(pe, a_pt, n - 2)
                    for h in range(HG):
                        last = pe.transpose(quads(bank(PTB))[:, h, :], dnorm[:, u % 2, h, :], idf[:, :])
                    last.then_inc(a_tp, 1)
                slot(1)
                if two:
                    w = (u - 2) % UN
                    pe.wait_ge(a_pt, n - 1)
                    wait(pe, a_o, n - 2)
                    pe.matmul(bank(OB), va[:, (w // CB) % 2, w % CB, :],
                              pt[:, u % 2, :, :], start=True, stop=True).then_inc(a_pv, 1)
                if not (first and u < 3):
                    pe.wait_ge(a_o, n - 2)
                    wait(pe, a_y, n - 3)
                    for h in range(HG):
                        last = pe.matmul(ps[:, YB, 0:DM], oa[:, (u - 3) % 2, h, :],
                                         wo[:, bass.ds((g if u >= 3 else g - 1) * HG + h, 1), :],
                                         start=h == 0, stop=h == HG - 1)
                    last.then_inc(a_wo, 1)

            pe.wait_ge(s_cst, 2)
            layer_norm(0)
            pe.wait_ge(a_wld, 64)
            pe.wait_ge(ln_l, NC * KT)
            for item in range(AN):
                a_project(0, 0, item, True)
            for u in range(UN):
                a_unit(0, u, first=True)
            with pe.Fori(1, NG) as g:
                for u in range(UN):
                    a_unit(g, u)
            for u in range(3):
                a_unit(NG, u, drain=True)

            def b_do(g_to, c, what, n):
                kind, t = what
                if kind == "qr":
                    q = (g_to * NC + c) * XP + t
                    pe.wait_ge(b_if, n + 1)
                    wait(pe, b_qs, q)
                    t0, t1, t2 = 3 * t, 3 * t + 1, 3 * t + 2
                    o = bank(QRB)
                    for m in range(2):
                        pe.matmul(o, mq[:, t1, m, :], qcs[:, t1, m, :], start=m == 0, stop=False,
                                  skip_group_check=True)
                    for m in range(2):
                        pe.matmul(o[0:64, :], mq[:, t0, m, 0:64], qcs[:, t0, m, :], start=False, stop=m == 1,
                                  skip_group_check=True)
                        last = pe.matmul(o[64:128, :], mq[:, t2, m, 64:128], qcs[:, t2, m, :], start=False,
                                         stop=m == 1, skip_group_check=True)
                    last.then_inc(b_qr, 1)
                    return
                bk = bank(2 + n_par(n))
                wait(pe, b_if, n - 1)
                if kind == "qb":
                    if c == 0:
                        pe.wait_ge(b_if, prep_of(g_to, t) + 1)
                    last = three_pass(bk, lambda kt: wbh[:, t, kt, :], lambda kt: wbl[:, t, kt, :], c)
                elif kind == "prep":
                    pe.wait_ge(b_raw_s, g_to * 16 + 16)
                    p, k = t // 3, t % 3
                    cols = {0: [(2 * p, 0, 128)], 1: [(2 * p, 128, 64), (2 * p + 1, 0, 64)],
                            2: [(2 * p + 1, 64, 128)]}[k]
                    for kt in range(KT):
                        at = 128 * kt
                        for h, a, w in cols:
                            pe.matmul(bk[:, at:at + w],
                                      raw_b[:, RB_WQ + h * DM + 128 * kt:RB_WQ + h * DM + 128 * (kt + 1)],
                                      raw_b[:, RB_KCQ + h * XQ + a:RB_KCQ + h * XQ + a + w], start=True, stop=True)
                            at += w
                    for m in range(2):
                        a = RB_QR + (2 * p + m) * 2 * XQ + 128 * k
                        last = pe.matmul(bk[:, 256 + 128 * m:384 + 128 * m], raw_b[:, a:a + 128],
                                         raw_b[:, RB_KR + 128 * p:RB_KR + 128 * (p + 1)], start=True, stop=True)
                else:
                    for i in range(2):
                        h = 2 * t + i
                        last = pe.matmul(bk[64 * i:64 * i + 64, 0:DM], raw_b[:, RB_KV + h * XC:RB_KV + (h + 1) * XC],
                                         raw_b[:, RB_WO + h * DM:RB_WO + (h + 1) * DM], start=True, stop=True)
                last.then_inc(b_it, 1)

            def n_par(n):
                return n % 2 if isinstance(n, int) else place[0] % 2
            place = [0]

            def prep_of(g_to, t):
                if isinstance(g_to, int) and g_to == 0:
                    return t
                slots = [k for k in B_PLACE if k[2] == ("prep", t)]
                return (g_to - 1) * BN + (BF + B_PLACE[slots[0]])

            def b_unit(g, u, first=False, drain=False):
                n, c, j = g * UN + u, u // CB, u % CB

                def slot(s):
                    if drain:
                        return
                    for what in b_slot(u, s):
                        ahead = c == NC - 1 or what[0] == "prep"
                        g_to = g + 1 if ahead and what[0] != "wco" else g
                        if what[0] == "qr":
                            item = b_last(g, u, s, "qb", 3 * what[1] + 2)
                        else:
                            item = b_item(g, u, s, what)
                            place[0] = B_PLACE[u, s, what]
                        b_do(g_to, (c + 1) % NC, what, item)
                slot(0)
                if not drain:
                    if j == 0:
                        pe.wait_ge(b_qs, (g * NC + (c + 1)) * XP)
                    wait(pe, b_ex, n - 1)
                    for p in range(XP):
                        last = pe.matmul(B_S[u % 2][:, 256 * p:256 * (p + 1)],
                                         qr[:, c % 2, p, S * j:S * (j + 1)], kbd[:, u, :, :], start=True, stop=True)
                    last.then_inc(b_sc, 1)
                two = not (first and u < 2) and not (drain and u >= 2)
                if two:
                    pe.wait_ge(b_dn, n - 1)
                    wait(pe, b_pt, n - 2)
                    for h in range(HG):
                        last = pe.transpose(quads(bank(PTB))[:, h, :], dnorm[:, u % 2, h, :], idf[:, :])
                    last.then_inc(b_tp, 1)
                slot(1)
                if two:
                    w = (u - 2) % UN
                    pe.wait_ge(b_pt, n - 1)
                    wait(pe, b_o, n - 2)
                    for i in range(2):
                        last = pe.matmul(ps[64 * i:64 * i + 64, OB, 0:XP * S], kvr[:, w, 0, :],
                                         pt[:, u % 2, i:HG:2, :], start=True, stop=True)
                    last.then_inc(b_pv, 1)
                if not (first and u < 3):
                    if u == 3:
                        pe.wait_ge(b_if, b_item(g, 2, 2, ("wco", 1)) + 1)
                    pe.wait_ge(b_o, n - 2)
                    wait(pe, b_y, n - 3)
                    for p in range(XP):
                        last = pe.matmul(ps[:, YB, 0:DM], ob[:, (u - 3) % 2, p, :], wco[:, p, :],
                                         start=p == 0, stop=p == XP - 1)
                    last.then_inc(b_wo, 1)
                slot(2)

            layer_norm(1)
            pe.wait_ge(b_kv, 5)
            for r in range(NC):
                if r >= 2:
                    pe.wait_ge(b_kvc, r - 1)
                for j in range(CB):
                    last = pe.transpose(quads(bank(4 + r % 2))[:, j, :], kvr[:, CB * r + j, :, :], idf[:, :])
                last.then_inc(b_kvp, 1)
            pe.wait_ge(ln_l, 2 * NC * KT)
            pe.wait_ge(b_kvc, NC)
            item = 0
            for what in B_FIRST:
                b_do(0, 0, what, item - 1 if what[0] == "qr" else item)
                item += what[0] != "qr"
            for u in range(UN):
                b_unit(0, u, first=True)
            with pe.Fori(1, NG) as g:
                for u in range(UN):
                    b_unit(g, u)
            for u in range(3):
                b_unit(NG, u, drain=True)

            layer_norm(2)
            pe.wait_ge(c_gws, 16)
            pe.wait_ge(ln_f, 3 * NC * KT)
            for b in range(B):
                for kt in range(KT):
                    last = pe.matmul(ps[:, 4, E * b:E * (b + 1)], xnf[:, kt, S * b:S * (b + 1)], gw[:, kt, :],
                                     start=kt == 0, stop=kt == KT - 1)
            last.then_inc(c_lg, 1)
            pe.wait_ge(c_gs, GATE_STEPS)
            for r in range(NC):
                tb = ps[0:KC, 5, :].bitcast(bf16)
                if r >= 1:
                    pe.wait_ge(c_cc, r)
                for j in range(CB):
                    last = pe.transpose(tb[:, S * j:S * (j + 1)], cmb[:, CB * r + j, :], idb[:, :])
                last.then_inc(c_ct, 1)
            pe.wait_ge(c_cc, NC)
            pe.wait_ge(ln_l, 3 * NC * KT)

            def c_down(v, g, c, t):
                pe.wait_ge(c_l, v + 1)
                if t == 0:
                    wait(pe, c_y, g * NC + c)
                par = (TG * c + t) % 2
                for j in range(CB):
                    for i, (h_, w_) in enumerate(((hhh, wch), (hhh, wcl), (hhl, wch))):
                        last = pe.matmul(ps[:, j // 2, DM * (j % 2):DM * (j % 2 + 1)],
                                         h_[:, par, S * j:S * (j + 1)], w_[:, t, 2 * KT * 128:RC_T],
                                         start=t == 0 and j % 2 == 0 and i == 0, stop=t == TG - 1 and i == 2,
                                         skip_group_check=True)
                last.then_inc(c_dn, 1)

            def c_unit(g, c, t, first=False):
                k = TG * c + t
                v = g * (NC * TG) + k
                if c == 0:
                    pe.wait_ge(c_lo, g * TG + (t + 1))
                tok = slice(CW * c, CW * (c + 1))
                wait(pe, c_sg, v - 1)
                three_pass(bank(C_G[k % 2]), lambda kt: wch[:, t, 128 * kt:128 * (kt + 1)],
                           lambda kt: wcl[:, t, 128 * kt:128 * (kt + 1)], c).then_inc(c_g, 1)
                wait(pe, c_hu, v - 1)
                three_pass(bank(C_U[k % 2]), lambda kt: wch[:, t, 256 + 128 * kt:384 + 128 * kt],
                           lambda kt: wcl[:, t, 256 + 128 * kt:384 + 128 * kt], c).then_inc(c_u, 1)
                wait(pe, c_h, v - 1)
                pe.matmul(bank(C_C[k % 2]), sel[:, t, :], combt[:, tok], start=True, stop=True).then_inc(c_c, 1)
                if not (first and k == 0):
                    c_down(v - 1, g if k else g - 1, ((k - 1) // TG) % NC, (k - 1) % TG)

            for c in range(NC):
                for t in range(TG):
                    c_unit(0, c, t, first=True)
            with pe.Fori(1, CG) as g:
                for c in range(NC):
                    for t in range(TG):
                        c_unit(g, c, t)
            c_down(CG * NC * TG - 1, CG - 1, NC - 1, TG - 1)

        @block.vector
        def _(dve):
            def layer_norm(stage):
                for c in range(NC):
                    m = stage * NC + c
                    if stage == 0:
                        dve.wait_ge(s_x[c], 16)
                    seqs = range(CB * c, CB * (c + 1))
                    for b in seqs:
                        last = dve.bn_stats(stats[:, b, :], x_sb[:, b, :])
                    last.then_inc(ln_st, 1)
                    dve.wait_ge(ln_st, m + 1)
                    for b in seqs:
                        last = dve.bn_aggr(mv[:, b, :], stats[:, b, :])
                    last.then_inc(ln_ag, 1)
                    dve.wait_ge(ln_ag, m + 1)
                    dve.tensor_scalar(veps[:, CB * c:CB * (c + 1)], mv[:, CB * c:CB * (c + 1), 1], LN_EPS, None,
                                      ALU.add).then_inc(ln_var, 1)

                def low(c):
                    for kt in range(KT):
                        dve.wait_ge(ln_h, 2 * (stage * NC + c) + kt + 1)
                        tok = slice(CW * c, CW * (c + 1))
                        dve.tensor_tensor(xnl[:, kt, tok], xnf[:, kt, tok], xnh[:, kt, tok].bitcast(f32),
                                          ALU.subtract).then_inc(ln_l, 1)
                for c in range(NC):
                    m = stage * NC + c
                    dve.wait_ge(ln_rs, m + 1)
                    if c >= 2:
                        dve.wait_ge(ln_tp, 2 * (m - 2) + 2)
                    for j in range(CB):
                        b = CB * c + j
                        last = dve.tensor_scalar(xnt[:, c % 2, j, :], x_sb[:, b, :], mv[:, b, 0:1], rstd[:, b:b + 1],
                                                 ALU.subtract, ALU.mult)
                    last.then_inc(ln_xt, 1)
                    if c >= 1:
                        low(c - 1)
                low(NC - 1)

            def a_take(g_to, c, item, between=lambda: None):
                chunk = g_to * NC + c
                if item == AV:
                    between()
                    return
                dve.wait_ge(a_pj, chunk * AN + (item + 1))
                src, par = quads(bank(PJ)), c % 2
                if item == 0:
                    to = ((k1[:, par, :], 2), (k2[:, par, :], 5))
                elif item == 1:
                    wait(dve, a_k, chunk)
                    to = ((ktmp[:, 0, :], 3), (ktmp[:, 1, :], 4))
                else:
                    h = item - 2
                    to = ((qa[:, par, h, :], 0), (qb[:, par, h, :], 1))
                for i, (dst, tab) in enumerate(to):
                    last = dve.tensor_tensor(quads(dst), src, bcast(taba[:, tab, :]), ALU.mult)
                    if i == 0:
                        between()
                last.then_inc(a_pf, 1)

            def a_rec2(n, par):
                dve.wait_ge(a_ex, n + 1)
                dve.reciprocal(rec2[:, par, :], sums[:, par, 4:8]).then_inc(a_r2, 1)

            def a_ratio(n, par):
                dve.wait_ge(a_r2, n + 1)
                dve.tensor_tensor(ratio[:, par, :], rec2[:, par, :], sums[:, par, 0:4], ALU.mult).then_inc(a_rt, 1)

            def a_rho(n, par, g):
                dve.wait_ge(a_rt, n + 1)
                dve.tensor_tensor(rho[:, par, :], ratio[:, par, :], nlam[:, bass.ds(g * HG, HG)], ALU.mult)\
                   .then_inc(a_rh, 1)

            def a_diff(n, par):
                dve.wait_ge(a_rh, n + 1)
                for h in range(HG):
                    last = dve.scalar_tensor_tensor(out=ea[:, par, 0, h, :], in0=ea[:, par, 1, h, :],
                                                    scalar=rho[:, par, h:h + 1], in1=ea[:, par, 0, h, :],
                                                    op0=ALU.mult, op1=ALU.add)
                last.then_inc(a_df, 1)

            def a_den(n, par):
                dve.wait_ge(a_re, n + 1)
                dve.scalar_tensor_tensor(out=den[:, par, :], in0=sums[:, par, 0:4], scalar=DIFF_EPS,
                                         in1=rsum[:, par, :], op0=ALU.mult, op1=ALU.add).then_inc(a_dd, 1)

            def a_rden(n, par):
                dve.wait_ge(a_dd, n + 1)
                dve.reciprocal(rden[:, par, :], den[:, par, :]).then_inc(a_cb, 1)

            def add_x(b, done, n, added):
                dve.wait_ge(done, n + 1)
                dve.tensor_tensor(x_sb[:, b, :], ps[:, YB, 0:DM], x_sb[:, b, :], ALU.add).then_inc(added, 1)

            def a_unit(g, u, first=False, drain=False):
                n, c, j = g * UN + u, u // CB, u % CB
                one = not (first and u < 1) and not (drain and u >= 1)
                two = not (first and u < 2) and not (drain and u >= 2)

                def slot(s, between):
                    if not drain and (j, s) in A_SLOT:
                        a_take(g + 1 if c == NC - 1 else g, (c + 1) % NC, A_SLOT[j, s], between)
                    else:
                        between()
                if two:
                    a_den(n - 2, u % 2)
                if not (first and u < 4):
                    add_x((u - 4) % UN, a_wo, n - 4, a_y)
                if two:
                    a_rden(n - 2, u % 2)
                if one:
                    a_rec2(n - 1, (u - 1) % 2)
                slot(0, (lambda: a_ratio(n - 1, (u - 1) % 2)) if one else (lambda: None))
                if one:
                    a_rho(n - 1, (u - 1) % 2, g if u else g - 1)
                    a_diff(n - 1, (u - 1) % 2)
                if not drain:
                    dve.wait_ge(a_sc, n + 1)
                    wait(dve, a_ex, n - 1)
                    dve.tensor_reduce(negmax[:, u % 2, :], A_S[u % 2].rearrange("p m (h k) -> p (m h) k", k=S),
                                      axis=AX.X, op=ALU.max, negate=True).then_inc(a_mx, 1)
                slot(1, lambda: None)

            dve.wait_ge(s_const, 32)
            dve.tensor_copy(idb[:, :], idf[:, :]).then_inc(s_cst, 1)
            dve.tensor_copy(maskb[:, :], maskf[:, :]).then_inc(s_cst, 1)
            layer_norm(0)
            dve.wait_ge(a_wld, 64)
            dve.tensor_scalar(nlam[:, :], nlam[:, :], -1.0, None, ALU.mult).then_inc(a_nl, 1)
            dve.wait_ge(a_nl, 1)
            for item in range(AN):
                a_take(0, 0, item)
            for u in range(UN):
                a_unit(0, u, first=True)
            with dve.Fori(1, NG) as g:
                for u in range(UN):
                    a_unit(g, u)
            for u in range(4):
                a_unit(NG, u, drain=True)

            def b_take(what, n, par, m_done):
                kind, t = what
                if kind == "qr":
                    return
                bk = bank(2 + par)
                dve.wait_ge(b_it, n + 1)
                if kind == "qb":
                    for m in range(2):
                        last = dve.tensor_tensor(quads(qcs[:, t, m, :]), quads(bk), bcast(tabb[:, t % 3, m, :]),
                                                 ALU.mult)
                elif kind == "prep":
                    dve.wait_ge(b_m, m_done + 1)
                    last = dve.tensor_tensor(wbl[:, t, :, :].rearrange("p k n -> p (k n)"), bk[:, 0:256],
                                             wbh[:, t, :, :].rearrange("p k n -> p (k n)").bitcast(f32), ALU.subtract)
                else:
                    last = dve.tensor_copy(wco[:, t, :], bk[:, 0:DM])
                last.then_inc(b_if, 1)

            def b_unit(g, u, first=False, drain=False):
                n = g * UN + u

                def slot(s):
                    if drain:
                        return
                    for what in b_slot(u, s):
                        if what[0] != "qr":
                            b_take(what, b_item(g, u, s, what), B_PLACE[u, s, what] % 2, (g + 1) * XT + what[1])
                slot(0)
                if not drain:
                    dve.wait_ge(b_sc, n + 1)
                    wait(dve, b_ex, n - 1)
                    dve.tensor_reduce(negmax[:, u % 2, 0:HG], quads(B_S[u % 2]), axis=AX.X, op=ALU.max,
                                      negate=True).then_inc(b_mx, 1)
                if not (first and u < 1) and not (drain and u >= 1):
                    par = (u - 1) % 2
                    dve.wait_ge(b_ex, n)
                    wait(dve, b_dn, n - 2)
                    dve.reciprocal(rsum[:, par, :], sums[:, par, 0:HG]).then_inc(b_rs, 1)
                slot(1)
                if not (first and u < 3):
                    add_x((u - 3) % UN, b_wo, n - 3, b_y)
                slot(2)

            a_over(dve)
            layer_norm(1)
            dve.wait_ge(b_ctx, 48)
            half = XC // 2
            dve.tensor_tensor(kvr[:, :, 0, :], kvin[:, :, :],
                              kvtab[:, 0, :].unsqueeze(1).broadcast_to([128, B, XC]), ALU.mult).then_inc(b_kv, 1)
            for d in (0, half):
                dve.tensor_tensor(kvt[:, :, d:d + half], kvin[:, :, half - d:XC - d],
                                  kvtab[:, 1, d:d + half].unsqueeze(1).broadcast_to([128, B, half]),
                                  ALU.mult).then_inc(b_kv, 1)
            dve.wait_ge(b_kv, 3)
            dve.tensor_tensor(kvr[:, :, 0, :], kvr[:, :, 0, :], kvt[:, :, :], ALU.add).then_inc(b_kv, 1)
            dve.wait_ge(b_kv, 4)
            dve.tensor_copy(kvr[:, :, 1, :], kvr[:, :, 0, :]).then_inc(b_kv, 1)
            dve.wait_ge(b_kz, 1)
            for r in range(NC):
                dve.wait_ge(b_kvp, r + 1)
                for i in range(2):
                    rows = slice(64 * i, 64 * i + 64)
                    last = dve.tensor_copy(kbd[rows, CB * r:CB * (r + 1), i, :], quads(bank(4 + r % 2))[rows])
                last.then_inc(b_kvc, 1)
            item = 0
            for what in B_FIRST:
                b_take(what, item, item % 2, what[1])
                item += what[0] != "qr"
            for u in range(UN):
                b_unit(0, u, first=True)
            with dve.Fori(1, NG) as g:
                for u in range(UN):
                    b_unit(g, u)
            for u in range(3):
                b_unit(NG, u, drain=True)

            b_over(dve)
            layer_norm(2)
            steps = [0]

            def step(ins):
                steps[0] += 1
                ins.then_inc(c_gs, 1)
                dve.wait_ge(c_gs, steps[0])

            def over_e(ap):
                return ap.unsqueeze(2).broadcast_to([128, B, E])
            logits = ps[:, 4, 0:B * E].rearrange("p (b e) -> p b e", e=E)
            dve.memset(cmb[:, :, :], 0.0)
            dve.memset(gone[:, :, :], 1.0)
            dve.wait_ge(c_lg, 1)
            step(dve.tensor_reduce(gmx[:, :], logits, axis=AX.X, op=ALU.max, negate=True))
            step(dve.tensor_tensor(gl[:, :, :], logits, over_e(gmx[:, :]), ALU.add))
            dve.memset(cmb[:, :, 3 * E:3 * E + 1], 1.0)
            dve.memset(gone[:, :, 0:1], 0.0)
            dve.wait_ge(c_ge, 1)
            step(dve.tensor_reduce(gsum[:, :], ge[:, :, :], axis=AX.X, op=ALU.add))
            step(dve.reciprocal(grec[:, :], gsum[:, :]))
            step(dve.tensor_tensor(gp[:, :, :], ge[:, :, :], over_e(grec[:, :]), ALU.mult))
            for b in range(B):
                last = dve.max(g8[:, b, :], gp[:, b, :])
            step(last)
            thr = g8[:, :, TOPK - 1:TOPK].broadcast_to([128, B, E])
            step(dve.tensor_tensor(ggt[:, :, :], gp[:, :, :], thr, ALU.is_gt))
            step(dve.tensor_tensor(geq[:, :, :], gp[:, :, :], thr, ALU.is_equal))
            step(dve.tensor_reduce(gn[:, :], ggt[:, :, :], axis=AX.X, op=ALU.add))
            step(dve.tensor_scalar(glim[:, :], gn[:, :], -1.0, float(TOPK), ALU.mult, ALU.add))
            flat = "p b e -> p (b e)"
            step(dve.tensor_tensor_scan(gcum[:, :, :].rearrange(flat), gone[:, :, :].rearrange(flat),
                                        geq[:, :, :].rearrange(flat), 0.0, ALU.mult, ALU.add))
            step(dve.tensor_tensor(gcum[:, :, :], gcum[:, :, :], over_e(glim[:, :]), ALU.is_le))
            step(dve.tensor_tensor(gcum[:, :, :], gcum[:, :, :], geq[:, :, :], ALU.mult))
            step(dve.tensor_tensor(gcum[:, :, :], gcum[:, :, :], ggt[:, :, :], ALU.add))
            step(dve.tensor_tensor(gp[:, :, :], gp[:, :, :], gcum[:, :, :], ALU.mult))
            step(dve.tensor_copy(cmb[:, :, 0:E], gp[:, :, :]))
            step(dve.tensor_tensor(gr1[:, :, :], gp[:, :, :], cmb[:, :, 0:E], ALU.subtract))
            step(dve.tensor_copy(cmb[:, :, E:2 * E], gr1[:, :, :]))
            step(dve.tensor_tensor(gr2[:, :, :], gr1[:, :, :], cmb[:, :, E:2 * E], ALU.subtract))
            step(dve.tensor_copy(cmb[:, :, 2 * E:3 * E], gr2[:, :, :]))
            assert steps[0] == GATE_STEPS

            def c_add(v, c, added):
                dve.wait_ge(c_dn, v + 1)
                for i in range(2):
                    dst = x_sb[:, CB * c + 2 * i:CB * c + 2 * i + 2, :].rearrange("p b d -> p (b d)")
                    last = dve.tensor_tensor(dst, bank(i), dst, ALU.add)
                last.then_inc(c_y, 1)

            def c_unit(g, c, t, first=False):
                k = TG * c + t
                v, par = g * (NC * TG) + k, k % 2
                dve.wait_ge(c_u, v + 1)
                dve.wait_ge(c_sg, v + 1)
                dve.tensor_tensor(hu[:, par, :], bank(C_U[par]), sg[:, par, :], ALU.mult).then_inc(c_hu, 1)
                dve.wait_ge(c_hu, v + 1)
                dve.wait_ge(c_c, v + 1)
                dve.tensor_tensor(hh[:, par, :], bank(C_C[par]), hu[:, par, :], ALU.mult).then_inc(c_h, 1)
                dve.wait_ge(c_hr, v + 1)
                dve.tensor_tensor(hhl[:, par, :], hh[:, par, :], hhh[:, par, :].bitcast(f32), ALU.subtract)\
                   .then_inc(c_l, 1)
                if t == 0 and not (first and k == 0):
                    c_add(v - 1, (c - 1) % NC, None)

            for c in range(NC):
                for t in range(TG):
                    c_unit(0, c, t, first=True)
            with dve.Fori(1, CG) as g:
                for c in range(NC):
                    for t in range(TG):
                        c_unit(g, c, t)
            c_add(CG * NC * TG - 1, NC - 1, None)

        @block.scalar
        def _(act):
            def copy(dst, src):
                return act.activation(dst, src, ACT.Copy)

            def layer_norm(stage):
                for c in range(NC):
                    for kt in range(KT):
                        m = 2 * (stage * NC + c) + kt
                        tok = slice(CW * c, CW * (c + 1))
                        act.wait_ge(ln_tp, m + 1)
                        copy(xnf[:, kt, tok], bank(2 * (c % 2) + kt)).then_inc(ln_f, 1)
                        act.wait_ge(ln_f, m + 1)
                        copy(xnh[:, kt, tok], xnf[:, kt, tok]).then_inc(ln_h, 1)

            def a_high(g_to, tile):
                act.wait_ge(a_raw, g_to * 16 + 16)
                t = slice(128 * tile, 128 * (tile + 1))
                copy(wah[:, :, t], raw_a[:, :, t]).then_inc(a_hi, 1)

            def a_take_v(g_to, c):
                act.wait_ge(a_pj, (g_to * NC + c) * AN + (AV + 1))
                copy(va[:, c % 2, :, :], quads(bank(PJ))).then_inc(a_pf, 1)

            def exps(n, u, maps, mx, ex, free, dst):
                par = u % 2
                act.wait_ge(mx, n + 1)
                wait(act, free, n - 1)
                for m in range(maps):
                    for h in range(HG):
                        i = m * HG + h
                        src = (A_S[par][:, m, :] if maps == 2 else B_S[par])
                        last = act.activation(dst(m, h), quads(src)[:, h, :], ACT.Exp, bias=negmax[:, par, i:i + 1],
                                              accum_out=sums[:, par, i:i + 1])
                last.then_inc(ex, 1)

            def a_unit(g, u, first=False, drain=False):
                n, c, j = g * UN + u, u // CB, u % CB

                def slot(s):
                    if drain or (j, s) not in A_SLOT:
                        return
                    item = A_SLOT[j, s]
                    if item == AV:
                        a_take_v(g + 1 if c == NC - 1 else g, (c + 1) % NC)
                    elif c == NC - 2:
                        act.wait_ge(a_pj, (g * NC + (NC - 1)) * AN + (item + 1))
                        a_high(g + 1, item)
                slot(0)
                two = not (first and u < 2) and not (drain and u >= 2)
                if two:
                    act.wait_ge(a_tp, n - 1)
                    wait(act, a_pv, n - 3)
                    copy(pt[:, u % 2, :, :], quads(bank(PTB))).then_inc(a_pt, 1)
                if not (first and u < 1) and not (drain and u >= 1):
                    act.wait_ge(a_df, n)
                    par = (u - 1) % 2
                    wait(act, a_dd, n - 2)
                    for h in range(HG):
                        last = act.activation(ea[:, par, 0, h, :], ea[:, par, 0, h, :], ACT.Relu,
                                              accum_out=rsum[:, par, h:h + 1])
                    last.then_inc(a_re, 1)
                if not drain:
                    exps(n, u, 2, a_mx, a_ex, a_dn, lambda m, h: ea[:, u % 2, m, h, :])
                slot(1)
                if two:
                    act.wait_ge(a_pv, n - 1)
                    wait(act, a_wo, n - 3)
                    copy(oa[:, (u - 2) % 2, :, :], quads(bank(OB))).then_inc(a_o, 1)

            layer_norm(0)
            for tile in range(AW):
                a_high(0, tile)
            a_take_v(0, 0)
            for u in range(UN):
                a_unit(0, u, first=True)
            with act.Fori(1, NG) as g:
                for u in range(UN):
                    a_unit(g, u)
            for u in range(2):
                a_unit(NG, u, drain=True)

            def b_take(g_to, c, what, n, par):
                kind, t = what
                if kind == "qr":
                    act.wait_ge(b_qr, (g_to * NC + c) * XP + (t + 1))
                    copy(qr[:, c % 2, t, :], bank(QRB)).then_inc(b_qs, 1)
                elif kind == "prep":
                    act.wait_ge(b_it, n + 1)
                    bk = bank(2 + par)
                    copy(wbh[:, t, :, :].rearrange("p k n -> p (k n)"), bk[:, 0:256])
                    copy(mq[:, t, :, :].rearrange("p k n -> p (k n)"), bk[:, 256:512]).then_inc(b_m, 1)

            def b_unit(g, u, first=False, drain=False):
                n, c = g * UN + u, u // CB

                def slot(s):
                    if drain:
                        return
                    for what in b_slot(u, s):
                        if what[0] in ("qr", "prep"):
                            item = None if what[0] == "qr" else b_item(g, u, s, what)
                            par = None if item is None else B_PLACE[u, s, what] % 2
                            b_take(g + 1 if c == NC - 1 else g, (c + 1) % NC, what, item, par)
                slot(0)
                two = not (first and u < 2) and not (drain and u >= 2)
                if two:
                    act.wait_ge(b_tp, n - 1)
                    wait(act, b_pv, n - 3)
                    copy(pt[:, u % 2, :, :], quads(bank(PTB))).then_inc(b_pt, 1)
                if not drain:
                    exps(n, u, 1, b_mx, b_ex, b_dn, lambda m, h: eb[:, u % 2, h, :])
                slot(1)
                if two:
                    act.wait_ge(b_pv, n - 1)
                    wait(act, b_wo, n - 3)
                    copy(ob[:, (u - 2) % 2, :, :].rearrange("p k n -> p (k n)"), ps[:, OB, 0:XP * S]).then_inc(b_o, 1)

            a_over(act)
            layer_norm(1)
            item = 0
            for what in B_FIRST:
                b_take(0, 0, what, item, item % 2)
                item += what[0] != "qr"
            for u in range(UN):
                b_unit(0, u, first=True)
            with act.Fori(1, NG) as g:
                for u in range(UN):
                    b_unit(g, u)
            for u in range(2):
                b_unit(NG, u, drain=True)

            def c_high(g_to, t):
                act.wait_ge(c_raw_s, g_to * 16 + 16)
                s0 = TG * RC_T + 128 * t
                copy(sel[:, t, :], raw_c[0:KC, s0:s0 + 128])
                copy(wch[:, t, :], raw_c[:, RC_T * t:RC_T * (t + 1)]).then_inc(c_hi, 1)

            b_over(act)
            layer_norm(2)
            for t in range(TG):
                c_high(0, t)
            act.wait_ge(c_gs, 2)
            act.activation(ge[:, :, :], gl[:, :, :], ACT.Exp).then_inc(c_ge, 1)
            for r in range(NC):
                act.wait_ge(c_ct, r + 1)
                copy(combt[:, CW * r:CW * (r + 1)], ps[0:KC, 5, :].bitcast(bf16)[:, 0:CW]).then_inc(c_cc, 1)

            def c_unit(g, c, t, first=False):
                k = TG * c + t
                v, par = g * (NC * TG) + k, k % 2
                act.wait_ge(c_g, v + 1)
                wait(act, c_hu, v - 1)
                act.activation(sg[:, par, :], bank(C_G[par]), ACT.Silu).then_inc(c_sg, 1)
                act.wait_ge(c_h, v + 1)
                wait(act, c_dn, v - 1)
                copy(hhh[:, par, :], hh[:, par, :]).then_inc(c_hr, 1)
                if (c == NC - 1 and t >= 1) or (k == 0 and not first):
                    act.wait_ge(c_dn, v)
                    c_high(g if k == 0 else g + 1, (t - 1) % TG)

            for c in range(NC):
                for t in range(TG):
                    c_unit(0, c, t, first=True)
            with act.Fori(1, CG) as g:
                for c in range(NC):
                    for t in range(TG):
                        c_unit(g, c, t)

        @block.gpsimd
        def _(pool):
            def layer_norm(stage):
                for c in range(NC):
                    m = stage * NC + c
                    cs = slice(CB * c, CB * (c + 1))
                    pool.wait_ge(ln_var, m + 1)
                    pool.tensor_tensor(rstd[:, cs], veps[:, cs], mhalf[:, cs], ALU.pow).then_inc(ln_rs, 1)

            def a_low(g_to, tile):
                pool.wait_ge(a_hi, g_to * AW + (tile + 1))
                t = slice(128 * tile, 128 * (tile + 1))
                pool.tensor_tensor(wal[:, :, t], raw_a[:, :, t], wah[:, :, t].bitcast(f32), ALU.subtract)\
                    .then_inc(a_lo, 1)

            def a_keys(g_to, c):
                pool.wait_ge(a_pf, (g_to * NC + c) * AN + 2)
                for m, k_ in enumerate((k1, k2)):
                    last = pool.tensor_tensor(k_[:, c % 2, :], k_[:, c % 2, :], ktmp[:, m, :], ALU.add)
                last.then_inc(a_k, 1)

            def norm(n, par, ready, done, free, src, rec):
                pool.wait_ge(ready, n + 1)
                wait(pool, free, n - 1)
                pool.tensor_tensor(dnorm[:, par, :, :], src[:, par, :, :],
                                   rec[:, par, :].unsqueeze(2).broadcast_to([128, HG, S]), ALU.mult).then_inc(done, 1)

            def a_unit(g, u, first=False, drain=False):
                n, c, j = g * UN + u, u // CB, u % CB
                if not (first and u < 2):
                    norm(n - 2, u % 2, a_cb, a_dn, a_tp, ea[:, :, 0, :, :], rden)
                if drain:
                    return
                if j == 0:
                    a_keys(g + 1 if c == NC - 1 else g, (c + 1) % NC)
                if c == NC - 2:
                    for s in range(2):
                        if (j, s) in A_SLOT and A_SLOT[j, s] != AV:
                            a_low(g + 1, A_SLOT[j, s])

            pool.memset(mhalf[:, :], -0.5).then_inc(s_cst2, 1)
            pool.wait_ge(s_cst2, 1)
            layer_norm(0)
            for tile in range(AW):
                a_low(0, tile)
            a_keys(0, 0)
            for u in range(UN):
                a_unit(0, u, first=True)
            with pool.Fori(1, NG) as g:
                for u in range(UN):
                    a_unit(g, u)
            for u in range(2):
                a_unit(NG, u, drain=True)

            a_over(pool)
            pool.memset(kbd[:, :, :, :], 0.0).then_inc(b_kz, 1)
            pool.wait_ge(b_kz, 1)
            layer_norm(1)
            for u in range(1, UN):
                norm(u - 1, (u - 1) % 2, b_rs, b_dn, b_tp, eb, rsum)
            with pool.Fori(1, NG) as g:
                for u in range(UN):
                    norm(g * UN + (u - 1), (u - 1) % 2, b_rs, b_dn, b_tp, eb, rsum)
            norm(NG * UN - 1, (UN - 1) % 2, b_rs, b_dn, b_tp, eb, rsum)

            def c_low(g_to, t):
                pool.wait_ge(c_hi, g_to * TG + (t + 1))
                pool.tensor_tensor(wcl[:, t, :], raw_c[:, RC_T * t:RC_T * (t + 1)], wch[:, t, :].bitcast(f32),
                                   ALU.subtract).then_inc(c_lo, 1)

            b_over(pool)
            layer_norm(2)
            for t in range(TG):
                c_low(0, t)
            with pool.Fori(1, CG) as g:
                for t in range(TG):
                    c_low(g, t)
            for t in range(TG - 1):
                c_low(CG, t)


_OUT = ((B, S, DM), "float32")


def _tables(np):
    f = np.float32
    pos = np.arange(S, dtype=f)

    def table(dim, rep):
        inv = (f(1.0) / np.power(f(10000.0), np.arange(0, dim, 2, dtype=f) / f(dim))).astype(f)
        ang = (pos[:, None] * inv[None, :]).astype(f).astype(np.float64)
        cos, sin = np.cos(ang), np.sin(ang)
        if rep:
            return np.repeat(cos, 2, axis=1), np.repeat(sin, 2, axis=1)
        return cos, sin
    c, s = (t.T for t in table(128, False))
    cc = lambda a, b: np.concatenate([a, b], axis=0)
    a_tab = np.stack([cc(c, s) / 8, cc(s, c) / 8, cc(c, -c), cc(-s, s), cc(c, c), cc(s, s)], axis=1)
    cq, sq = (t.T for t in table(XQ, True))
    half = XQ // 2
    sq = np.concatenate([sq[half:], -sq[:half]], axis=0)
    b_tab = np.stack([np.tile(cq, (2, 1)).reshape(3, 128, S), np.tile(sq, (2, 1)).reshape(3, 128, S)])
    b_tab = b_tab.transpose(2, 1, 0, 3)
    ck, sk = table(XC, True)
    sk = np.concatenate([-sk[:, :XC // 2], sk[:, XC // 2:]], axis=1)
    kv = np.stack([ck, sk], axis=1)
    q, k = np.arange(S)[:, None], np.arange(S)[None, :]
    mask = np.where((k <= q) & (k >= q - WINDOW + 1), 0.0, NEG)
    sel = np.zeros((CG + 1, 128, TG, 128))
    for g in range(CG + 1):
        for t in range(TG):
            for i in range(128):
                e = ((g % CG) * TG + t) * 128 + i
                rows = [e // EI + E * m for m in range(3)] if e < E * EI else [3 * E]
                sel[g, rows, t, i] = 1.0
    to = lambda a: np.ascontiguousarray(a.astype(f))
    return to(a_tab), to(b_tab), to(kv), to(mask), to(np.eye(128)), sel.astype(f)


def kernel(**inputs):
    import numpy as np
    import concourse.bacc as _bacc
    from concourse.bass_utils import run_bass_kernel_spmd as _run

    w = {k: np.asarray(v) for k, v in inputs.items()}
    a_tab, b_tab, kvtab, mask, ident, sel = _tables(np)
    f = np.float32

    def rows(a):
        return a.reshape(KT, 128, -1).transpose(1, 0, 2)

    def again(a):
        return np.concatenate([a, a[:1]], axis=0)
    wq, wk, wv = w["L0_attn_Wq"], w["L0_attn_Wk"], w["L0_attn_Wv"]
    a_wqk = []
    for g in range(NG):
        k = wk[:, 128 * g:128 * (g + 1)]
        a_wqk.append(rows(np.concatenate([k[:, :64], k[:, :64], k[:, 64:], k[:, 64:],
                                          wq[:, 512 * g:512 * (g + 1)]], axis=1)))
    a_wv = rows(np.concatenate([wv, wv[:, :128]], axis=1))
    a_wo = w["L0_attn_Wo"].reshape(H, 128, DM).transpose(1, 0, 2)
    a_lam = np.broadcast_to(w["L0_attn_lam"][None, :], (128, H))

    xq = w["L0_xattn_Wq"].reshape(H, 128, DM)
    kcq, kckv = w["L0_xattn_w_kc_q"], w["L0_xattn_w_kc_kv"]
    wqr, wkr = w["L0_xattn_W_qr"], w["L0_xattn_W_kr"]
    xwo = w["L0_xattn_Wo"].T.reshape(H, 128, DM)
    b_raw = np.zeros((NG, 128, RB_N), f)
    for g in range(NG):
        for i in range(HG):
            h, p = HG * g + i, i // 2
            half = slice(64 * (i % 2), 64 * (i % 2) + 64)
            b_raw[g, :, RB_WQ + i * DM:RB_WQ + (i + 1) * DM] = xq[h]
            b_raw[g, :, RB_KCQ + i * XQ:RB_KCQ + (i + 1) * XQ] = kcq[h]
            b_raw[g, :, RB_KV + i * XC:RB_KV + (i + 1) * XC] = kckv[h]
            b_raw[g, :, RB_WO + i * DM:RB_WO + (i + 1) * DM] = xwo[h]
            b_raw[g, half, RB_KR + 128 * p + 64 * (i % 2):RB_KR + 128 * p + 64 * (i % 2) + 64] = wkr[h].T
            for m, rolled in enumerate((wqr[h], np.roll(wqr[h], -(XQ // 2), axis=0))):
                a = RB_QR + (2 * p + m) * 2 * XQ + XQ * (i % 2)
                b_raw[g, half, a:a + XQ] = rolled.T

    def hidden(moe, shared, r0, r1, s0, s1):
        a = np.zeros((IT * 128, DM), f)
        a[:E * EI] = moe[:, r0:r1].reshape(E * EI, DM)
        a[E * EI:E * EI + SI] = shared[s0:s1]
        return a
    w1, s1 = w["L0_ffn_w1"], w["L0_ffn_shared_w1"]
    gu = np.stack([hidden(w1, s1, 0, EI, 0, SI), hidden(w1, s1, EI, 2 * EI, SI, 2 * SI)])
    gu = gu.reshape(2, CG, TG, 128, KT, 128).transpose(1, 5, 2, 0, 4, 3).reshape(CG, 128, TG, 2 * KT * 128)
    dn = hidden(w["L0_ffn_w2"].transpose(0, 2, 1), w["L0_ffn_shared_w2"].T, 0, EI, 0, SI)
    dn = dn.reshape(CG, TG, 128, DM).transpose(0, 2, 1, 3)
    c_raw = again(np.concatenate([gu, dn], axis=3).reshape(CG, 128, TG * RC_T))
    c_raw = np.concatenate([c_raw, sel.reshape(CG + 1, 128, TG * 128)], axis=2)
    c_gate = rows(w["L0_ffn_gate_w"].T)

    nc = _bacc.Bacc("TRN2", target_bir_lowering=False, num_devices=1)
    given = dict(x=w["x"], ctx_in=w["ctx_512"], in_wqk=again(np.stack(a_wqk)), in_wv=a_wv, in_wo=a_wo,
                 in_lam=a_lam, in_taba=a_tab, in_rawb=again(b_raw), in_tabb=b_tab, in_kvtab=kvtab, in_rawc=c_raw,
                 in_gate=c_gate, ident=ident, mask=mask)
    arrays, args = {}, {}
    for name, a in given.items():
        a = np.ascontiguousarray(a)
        arrays[f"{name}_dram"] = a
        args[name] = nc.dram_tensor(f"{name}_dram", a.shape, mybir.dt.from_np(a.dtype), kind="ExternalInput").ap()
    shape, dtype = _OUT
    args["out"] = nc.dram_tensor("out_0", shape, mybir.dt.from_np(np.dtype(dtype)), kind="ExternalOutput").ap()
    decoder_kernel(nc, **args)
    r = _run(nc, [arrays], core_ids=[0])
    return r.results[0]["out_0"]
```

```python
import concourse.bass as bass
from concourse import mybir
from contextlib import ExitStack

B, S, DM = 16, 128, 256
KT = DM // 128
CB = 4
NC = B // CB
CW = CB * S
H, HG = 16, 4
NG = H // HG
UN = B
WINDOW = 64
LN_EPS = 1e-5
DIFF_EPS = 1e-6
NEG = -1e30
XQ, XC = 192, 64
XT = HG * XQ // 128
XP = HG // 2
E, EI, SI, TOPK = 16, 176, 352, 6
IT = (E * EI + 384) // 128
TG = 5
CG = IT // TG
KC = 64

RB_WQ, RB_KCQ = 0, HG * DM
RB_QR = RB_KCQ + HG * XQ
RB_KR = RB_QR + XP * 2 * 2 * XQ
RB_KV = RB_KR + XP * 128
RB_WO = RB_KV + HG * XC
RB_N = RB_WO + HG * DM

GATE_STEPS = 21
GP = 2
GB = B // GP

RC_T = 2 * KT * 128 + DM
RC_N = TG * RC_T + TG * 128


def wait(eng, sem, value):
    if isinstance(value, int) and value <= 0:
        return
    eng.wait_ge(sem, value)


def decoder_kernel(nc, x, ctx_in, in_wqk, in_wv, in_wo, in_lam, in_taba, in_rawb, in_tabb, in_kvtab,
                   in_rawc, in_gate, ident, mask, out):
    f32, f32r, bf16 = mybir.dt.float32, mybir.dt.float32r, mybir.dt.bfloat16
    ALU, ACT, AX = mybir.AluOpType, mybir.ActivationFunctionType, mybir.AxisListType
    ctx = ExitStack()

    def sem(name):
        return ctx.enter_context(nc.semaphore(name))

    def sb(stack, name, shape, dt=f32):
        return stack.enter_context(nc.sbuf_tensor(name, shape, dt))

    with ctx:
        x_sb = sb(ctx, "x_sb", [128, B, DM])
        xnf = sb(ctx, "xnf", [128, KT, B * S])
        xnh = sb(ctx, "xnh", [128, KT, B * S], f32r)
        xnl = sb(ctx, "xnl", [128, KT, B * S], f32r)
        xnt = sb(ctx, "xnt", [128, 2, CB, DM])
        stats = sb(ctx, "stats", [128, B, 6])
        mv = sb(ctx, "mv", [128, B, 2])
        veps = sb(ctx, "veps", [128, B])
        rstd = sb(ctx, "rstd", [128, B])
        mhalf = sb(ctx, "mhalf", [128, B])
        idf = sb(ctx, "idf", [128, 128])
        idb = sb(ctx, "idb", [128, 128], bf16)
        maskf = sb(ctx, "maskf", [128, 128])
        maskb = sb(ctx, "maskb", [128, 128], bf16)
        raw_w = sb(ctx, "raw_w", [128, max(RB_N, RC_N)])
        raw_b, raw_c = raw_w[:, 0:RB_N], raw_w[:, 0:RC_N]
        wo = raw_w[:, 0:H * DM].rearrange("p (h d) -> p h d", d=DM)
        gw = sb(ctx, "gw", [128, KT, E])
        negmax = sb(ctx, "negmax", [128, 2, 8])
        sums = sb(ctx, "sums", [128, 2, 8])
        rec2 = sb(ctx, "rec2", [128, 2, 4])
        ratio = sb(ctx, "ratio", [128, 2, 4])
        rho = sb(ctx, "rho", [128, 2, 4])
        rsum = sb(ctx, "rsum", [128, 2, 4])
        den = sb(ctx, "den", [128, 2, 4])
        rden = sb(ctx, "rden", [128, 2, 4])
        pt = sb(ctx, "pt", [128, 2, HG, S])

        am = ExitStack()
        raw_a = sb(am, "raw_a", [128, KT, 768])
        wah = sb(am, "wah", [128, KT, 768], f32r)
        wal = sb(am, "wal", [128, KT, 768], f32r)
        wv = sb(am, "wv", [128, KT, NG * 128])
        taba = sb(am, "taba", [128, 6, S])
        ktmp = sb(am, "ktmp", [128, 2, CW])
        sb(am, "a_gap", [128, 256])
        woh = sb(am, "woh", [128, HG, DM], f32r)
        wol = sb(am, "wol", [128, HG, DM], f32r)
        qab = sb(am, "qab", [128, 2, 2, HG, CW])
        ea = sb(am, "ea", [128, 2, 2, HG, S])
        kva = sb(am, "kva", [128, 2, 3, CW])
        oah = sb(am, "oah", [128, 2, HG, S], f32r)
        oal = sb(am, "oal", [128, 2, HG, S], f32r)
        nlam = sb(am, "nlam", [128, H])
        am.close()
        bm = ExitStack()
        wbh = sb(bm, "wbh", [128, XT, KT, 128], f32r)
        wbl = sb(bm, "wbl", [128, XT, KT, 128], f32r)
        mq = sb(bm, "mq", [128, XT, 2, 128])
        kvin = sb(bm, "kvin", [128, B, XC])
        tabb = sb(bm, "tabb", [128, 3, 2, S])
        kvt = sb(bm, "kvt", [128, B, XC])
        kvtab = sb(bm, "kvtab", [128, 2, XC])
        sb(bm, "b_gap1", [128, 128])
        qr = sb(bm, "qr", [128, 2, XP, CW])
        kbd = sb(bm, "kbd", [128, B, 2, S])
        qcs = sb(bm, "qcs", [128, XT, 2, CW])
        eb = sb(bm, "eb", [128, 2, HG, S])
        obh = sb(bm, "obh", [128, 2, XP, S], f32r)
        obl = sb(bm, "obl", [128, 2, XP, S], f32r)
        wcoh = sb(bm, "wcoh", [128, XP, DM], f32r)
        wcol = sb(bm, "wcol", [128, XP, DM], f32r)
        sb(bm, "b_gap2", [128, 2 * 1024 + 16])
        kvr = sb(bm, "kvr", [128, B, 2, XC])
        bm.close()
        cm = ExitStack()
        wch = sb(cm, "wch", [128, TG, RC_T], f32r)
        wcl = sb(cm, "wcl", [128, TG, RC_T], f32r)
        sg = sb(cm, "sg", [128, 2, CW])
        hu = sb(cm, "hu", [128, 2, CW])
        hh = sb(cm, "hh", [128, 2, CW])
        hhh = sb(cm, "hhh", [128, 2, CW], f32r)
        hhl = sb(cm, "hhl", [128, 2, CW], f32r)
        sb(cm, "c_gap", [128, 1024])
        combt = sb(cm, "combt", [KC, B * S], bf16)
        cmb = sb(cm, "cmb", [128, B, KC], bf16)
        sel = sb(cm, "sel", [KC, TG, 128], bf16)
        gl = sb(cm, "gl", [128, B, E])
        ge = sb(cm, "ge", [128, B, E])
        gp = sb(cm, "gp", [128, B, E])
        g8 = sb(cm, "g8", [128, B, 8])
        ggt = sb(cm, "ggt", [128, B, E])
        geq = sb(cm, "geq", [128, B, E])
        gcum = sb(cm, "gcum", [128, B, E])
        gone = sb(cm, "gone", [128, B, E])
        gr1 = sb(cm, "gr1", [128, B, E])
        gr2 = sb(cm, "gr2", [128, B, E])
        gmx = sb(cm, "gmx", [128, B])
        gsum = sb(cm, "gsum", [128, B])
        grec = sb(cm, "grec", [128, B])
        gn = sb(cm, "gn", [128, B])
        glim = sb(cm, "glim", [128, B])
        cm.close()

        ps = ctx.enter_context(nc.psum_tensor("ps", [128, 8, 512], f32))

        def bank(n):
            return ps[:, n, :]

        def quads(ap):
            return ap.rearrange("p (h k) -> p h k", k=S)

        s_x = [sem(f"x_loaded{c}") for c in range(NC)]
        s_const, s_mask, s_cst = sem("identity_loaded"), sem("mask_loaded"), sem("const_ready")
        ln_st, ln_ag, ln_var = sem("ln_stats"), sem("ln_aggr"), sem("ln_var")
        ln_rs, ln_xt = sem("ln_rstd"), sem("ln_token_major")
        ln_tp, ln_f = sem("ln_transposed"), sem("ln_feature_major")
        ln_h, ln_l, ln_l2 = sem("ln_high"), sem("ln_low_first_tile"), sem("ln_low_second_tile")
        a_raw, a_tab = sem("a_raw_loaded"), sem("a_tables_loaded")
        a_wvl, a_wld = sem("a_wv_loaded"), sem("a_weights_loaded")
        a_hi, a_lo = sem("a_w_high"), sem("a_w_low")
        a_vf = sem("a_values_taken")
        a_pj, a_pf, a_k = sem("a_projected"), sem("a_projection_taken"), sem("a_k_ready")
        a_sc, a_mx, a_ex = sem("a_scores"), sem("a_negmax"), sem("a_exp")
        a_r2, a_rt, a_rh = sem("a_rec2"), sem("a_ratio"), sem("a_rho")
        a_df, a_re, a_dd = sem("a_difference"), sem("a_clipped"), sem("a_denominator")
        a_cb, a_dn = sem("a_norm_ready"), sem("a_weights_normed")
        a_tp, a_pt, a_pv = sem("a_transposed"), sem("a_pt_ready"), sem("a_pv")
        a_woh, a_wol, a_ol = sem("a_wo_high"), sem("a_wo_low"), sem("a_o_low")
        a_o, a_wo, a_y, a_nl = sem("a_o_high"), sem("a_out"), sem("a_x_added"), sem("a_nlam_ready")
        b_raw_s, b_ctx = sem("b_raw_loaded"), sem("b_ctx_loaded")
        b_kv, b_kz = sem("b_kv_step"), sem("b_kv_zeroed")
        b_kvp, b_kvc = sem("b_kv_transposed"), sem("b_kv_block")
        b_it, b_if, b_m = sem("b_item_done"), sem("b_item_taken"), sem("b_high_and_m_ready")
        b_qr, b_qs = sem("b_qr"), sem("b_qr_ready")
        b_sc, b_mx, b_ex = sem("b_scores"), sem("b_negmax"), sem("b_exp")
        b_rs, b_dn = sem("b_rsum"), sem("b_weights_normed")
        b_tp, b_pt, b_pv = sem("b_transposed"), sem("b_pt_ready"), sem("b_pv")
        b_wh, b_ol = sem("b_wco_high"), sem("b_o_low")
        b_o, b_wo, b_y = sem("b_o_high"), sem("b_out"), sem("b_x_added")
        c_raw_s = sem("c_raw_loaded")
        c_hi, c_lo = sem("c_w_high"), sem("c_w_low")
        c_lg, c_gs, c_ge = sem("c_logits"), sem("c_gate_step"), sem("c_gate_exp")
        c_ct, c_cc = sem("c_comb_transposed"), sem("c_comb_ready")
        c_z, c_g, c_u, c_c = sem("c_gate_constants"), sem("c_gate_done"), sem("c_up_done"), sem("c_comb_spread")
        c_sg, c_hu, c_h = sem("c_silu"), sem("c_silu_up"), sem("c_hidden_ready")
        c_hr, c_l = sem("c_hidden_high"), sem("c_hidden_low")
        c_dn, c_y = sem("c_down_done"), sem("c_x_added")
        s_out, s_cst2, c_gws = sem("out_stored"), sem("mhalf_ready"), sem("c_gate_weights_loaded")
        block = ctx.enter_context(nc.Block())

        A_ITEMS = ["k", "k'", "q0", "q1", "v", "q2", "q3"]
        AN, AV = len(A_ITEMS), A_ITEMS.index("v")
        A_SLOT = {(0, 0): 0, (0, 1): 1, (1, 0): 2, (1, 1): 3, (2, 0): 4, (2, 1): 5, (3, 1): 6}
        AW = AN - 1
        A_EXTRA = {("first", 3, 0): [("ln", 3, 0)], ("first", 7, 0): [("ln", 3, 1)],
                   ("final", 11, 0): [("ln", 4, 0)], ("final", 11, 1): [("ln", 4, 1)],
                   ("final", 12, 0): [("prep", 0)], ("final", 12, 1): [("prep", 1)],
                   ("final", 13, 0): [("prep", 2)], ("final", 13, 1): [("prep", 3)], ("final", 13, 2): [("prep", 4)],
                   ("final", 14, 0): [("prep", 5)], ("final", 14, 1): [("ln", 5, 0)], ("final", 14, 2): [("ln", 5, 1)],
                   ("final", 15, 1): [("kbd", 0)], ("final", 15, 2): [("kbd", 1)],
                   ("drain", 0, 1): [("qb", 0), ("qb", 1), ("kbd", 2)], ("drain", 0, 2): [("kbd", 3)],
                   ("drain", 1, 0): [("ln", 6, 0)], ("drain", 1, 1): [("qb", 2), ("qb", 3)],
                   ("drain", 1, 2): [("ln", 6, 1)]}

        def a_part(first, final, drain):
            return "first" if first else "final" if final else "drain" if drain else ""

        def a_tile(item):
            return item - (item > AV)
        A_START, A_TURNS = [[0, 1, 2, 3], [4, 5, 6]], 4

        def bcast(tab):
            return tab.unsqueeze(1).broadcast_to([128, CB, S])

        B_STEP = [("qb", 0), ("qb", 1), ("qb", 2), ("qb", 3), ("qr", 0), ("qb", 4), ("qb", 5), ("qr", 1)]
        B_PREP = {(10, 1): 0, (11, 0): 1, (11, 1): 2, (12, 0): 3, (12, 1): 4, (13, 0): 5}

        def b_slot(u, s, final=False):
            if final and u >= UN - CB:
                return []
            if final and s < 2:
                return [B_STEP[2 * (u % CB) + s]]
            if s == 2:
                return [("wco", 0), ("wco", 1)] if u == 2 else []
            return [B_STEP[2 * (u % CB) + s]] + ([("prep", B_PREP[u, s])] if (u, s) in B_PREP else [])

        B_PLACES = {False: {}, True: {}}
        for final_, places_ in B_PLACES.items():
            for u_ in range(UN):
                for s_ in range(3):
                    for what_ in b_slot(u_, s_, final_):
                        if what_[0] != "qr":
                            places_[u_, s_, what_] = len(places_)
        B_PLACE = B_PLACES[False]
        BN = len(B_PLACE)

        def b_places(g):
            return B_PLACES[isinstance(g, int) and g == NG - 1]
        B_FIRST = [("prep", t) for t in range(XT)] + B_STEP
        BF = 2 * XT
        assert BN % 2 == 0 and BF % 2 == 0

        def b_item(g, u, s, what):
            return g * BN + (BF + b_places(g)[u, s, what])

        def b_last(g, u, s, kind, t):
            ahead = [n for k, n in b_places(g).items() if k[2] == (kind, t) and (k[0], k[1]) <= (u, s)]
            if ahead:
                return g * BN + (BF + max(ahead))
            return (g - 1) * BN + (BF + max(B_PLACE[k] for k in B_PLACE if k[2] == (kind, t)))

        A_S, B_S = [ps[:, 0:2, :], ps[:, 2:4, :]], [ps[:, 0, :], ps[:, 1, :]]
        PTB, OB, YB, PJ, QRB = 4, 5, 6, 7, 7
        C_G, C_U, C_C = [2, 3], [4, 5], [6, 7]

        def ln_bank(c, kt):
            return 2 * (c % 2) + kt

        def a_over(eng):
            eng.wait_ge(a_y, NG * UN)

        B_EXTRA = {("final", 12, 0): [("ln", 8, 0, 2), ("ln", 8, 1, 3)],
                   ("final", 12, 1): [("ln", 9, 0, 7), ("ln", 9, 1, 2)],
                   ("final", 13, 0): [("logits", 0, 3)],
                   ("drain", 0, 2): [("ln", 10, 0, 2), ("ln", 10, 1, 3)],
                   ("drain", 1, 2): [("comb", 0, 7), ("comb", 1, 0)]}

        @block.sync
        def _(sp):
            for c in range(NC):
                if c == 0:
                    sp.dma_start(idf[:, :], ident).then_inc(s_const, 16)
                sp.dma_start(x_sb[:, CB * c:CB * (c + 1), :],
                             x[CB * c:CB * (c + 1)].rearrange("b p d -> p b d")).then_inc(s_x[c], 16)
                if c == 0:
                    sp.dma_start(raw_a[:, :, :], in_wqk[0]).then_inc(a_raw, 16)
                if c == 1:
                    sp.dma_start(taba[:, :, :], in_taba).then_inc(a_tab, 16)
                    sp.dma_start(maskf[:, :], mask).then_inc(s_mask, 16)
                    sp.dma_start(wv[:, :, :], in_wv).then_inc(a_wvl, 16)
            sp.dma_start(nlam[:, :], in_lam).then_inc(a_wld, 16)
            sp.dma_start(wo[:, :, :], in_wo).then_inc(a_wld, 16)
            with sp.Fori(0, NG - 1) as g:
                sp.wait_ge(a_lo, g * AW + AW)
                sp.dma_start(raw_a[:, :, :], in_wqk[bass.ds(g + 1, 1)].rearrange("o p k n -> p (o k) n"))\
                  .then_inc(a_raw, 16)
            sp.wait_ge(a_woh, NG)
            sp.wait_ge(a_wol, NG)
            sp.dma_start(raw_b[:, :], in_rawb[0]).then_inc(b_raw_s, 16)
            sp.wait_ge(a_vf, NG * NC)
            sp.wait_ge(a_pf, NG * NC * AW)
            sp.wait_ge(a_k, NG * NC)
            sp.dma_start(kvin[:, :, :], ctx_in.rearrange("b p d -> p b d")).then_inc(b_ctx, 16)
            sp.dma_start(kvtab[:, :, :], in_kvtab).then_inc(b_ctx, 16)
            sp.dma_start(tabb[:, :, :, :], in_tabb).then_inc(b_ctx, 16)
            sp.dma_start(gw[:, :, :], in_gate).then_inc(c_gws, 16)
            with sp.Fori(0, NG - 1) as g:
                sp.wait_ge(b_if, g * BN + (BF + B_PLACE[2, 2, ("wco", 1)] + 1))
                sp.dma_start(raw_b[:, :], in_rawb[bass.ds(g + 1, 1)].rearrange("o p n -> p (o n)"))\
                  .then_inc(b_raw_s, 16)
            sp.wait_ge(b_if, b_item(NG - 1, 2, 2, ("wco", 1)) + 1)
            sp.dma_start(raw_c[:, :], in_rawc[0]).then_inc(c_raw_s, 16)
            with sp.Fori(0, CG) as g:
                sp.wait_ge(c_lo, g * TG + TG)
                sp.dma_start(raw_c[:, :], in_rawc[bass.ds(g + 1, 1)].rearrange("o p n -> p (o n)"))\
                  .then_inc(c_raw_s, 16)
            for c in range(NC):
                sp.wait_ge(c_y, (CG - 1) * NC + c + 1)
                sp.dma_start(out[CB * c:CB * (c + 1)].rearrange("b p d -> p b d"),
                             x_sb[:, CB * c:CB * (c + 1), :]).then_inc(s_out, 16)
            sp.wait_ge(c_raw_s, 16 * (CG + 1))
            sp.wait_ge(s_out, 16 * NC)

        @block.tensor
        def _(pe):
            def three_pass(out_ap, wh, wl, c):
                tok = slice(CW * c, CW * (c + 1))
                steps = [(w(kt), m[:, kt, tok]) for kt in range(KT) for w, m in ((wh, xnh), (wh, xnl), (wl, xnh))]
                for n, (w, m) in enumerate(steps):
                    last = pe.matmul(out_ap, w, m, start=n == 0, stop=n == len(steps) - 1)
                return last

            def ln_turn(m, kt, bk):
                pe.wait_ge(ln_xt, m + 1)
                for j in range(CB):
                    last = pe.transpose(quads(bank(bk))[:, j, :], xnt[:, m % 2, j, 128 * kt:128 * (kt + 1)], idf[:, :])
                last.then_inc(ln_tp, 1)

            def ln_ready(m):
                pe.wait_ge(ln_l, m + 1)
                pe.wait_ge(ln_l2, m + 1)

            def layer_norm(stage):
                for c in range(NC):
                    for kt in range(KT):
                        if c >= 2:
                            pe.wait_ge(ln_h, 2 * (stage * NC + c - 2) + kt + 1)
                        ln_turn(stage * NC + c, kt, ln_bank(c, kt))

            held = []

            def pj_taken(what):
                if what[0] == "ln":
                    pe.wait_ge(ln_h, 2 * what[1] + what[2] + 1)
                elif what[0] == "prep":
                    pe.wait_ge(b_if, what[1] + 1)
                else:
                    pe.wait_ge(b_kvc, what[1] + 1)

            def b_turn(r):
                pe.wait_ge(b_kv, 5)
                for j in range(CB):
                    last = pe.transpose(quads(bank(PJ))[:, j, :], kvr[:, CB * r + j, :, :], idf[:, :])
                last.then_inc(b_kvp, 1)

            def a_project(g_to, c, item, fresh, turns=1):
                if turns > 1:
                    wait(pe, a_pf, item + 1 - turns)
                elif item == AV + 1:
                    pe.wait_ge(a_vf, (g_to * NC + c) + 1)
                elif item == 0 and AV == AN - 1:
                    pe.wait_ge(a_vf, g_to * NC + c)
                else:
                    wait(pe, a_pf, (g_to * NC + c) * AW + a_tile(item))
                to = PJ - (item % turns if turns > 1 else 0)
                if item == AV:
                    for j in range(CB):
                        tok = slice(S * (CB * c + j), S * (CB * c + j + 1))
                        for kt in range(KT):
                            last = pe.matmul(quads(bank(to))[:, j, :], xnf[:, kt, tok],
                                             wv[:, kt, bass.ds(g_to * 128, 128)], start=kt == 0, stop=kt == KT - 1)
                else:
                    if fresh:
                        pe.wait_ge(a_lo, g_to * AW + (a_tile(item) + 1))
                    t = slice(128 * a_tile(item), 128 * a_tile(item) + 128)
                    last = three_pass(bank(to), lambda kt: wah[:, kt, t], lambda kt: wal[:, kt, t], c)
                last.then_inc(a_pj, 1)

            def a_unit(g, u, first=False, final=False, drain=False):
                n, c, j = g * UN + u, u // CB, u % CB

                def slot(s):
                    if not drain and (j, s) in A_SLOT and not (final and c == NC - 1):
                        ahead = c == NC - 1
                        if held:
                            pj_taken(held.pop())
                        if first and not ahead and A_SLOT[j, s] == 0:
                            ln_ready(c + 1)
                        a_project(g + 1 if ahead else g, (c + 1) % NC, A_SLOT[j, s], ahead)
                    for what in A_EXTRA.get((a_part(first, final, drain), u, s), []):
                        if what[0] == "qb":
                            if what[1] == 0:
                                pe.wait_ge(a_ex, NG * UN)
                                ln_ready(NC)
                            b_do(0, 0, what, BF // 2 + what[1])
                            continue
                        if held:
                            pj_taken(held.pop())
                        else:
                            ahead = [i for k, i in A_SLOT.items() if k <= (j, s)]
                            if final and c == NC - 1:
                                ahead = []
                            pe.wait_ge(a_pf, (g * NC + (c + 1)) * AW + len([i for i in ahead if i != AV]))
                            pe.wait_ge(a_vf, g * NC + (c + 1) + (AV in ahead))
                        if what[0] == "ln":
                            ln_turn(what[1], what[2], PJ)
                        elif what[0] == "prep":
                            b_prep(0, what[1], bank(PJ)).then_inc(b_it, 1)
                        else:
                            b_turn(what[1])
                        held.append(what)
                slot(0)
                if first and u == 1:
                    for kt in range(KT):
                        ln_turn(2, kt, PTB + kt)
                if not drain:
                    if j == 0:
                        pe.wait_ge(a_pf, (g * NC + (c + 1)) * AW)
                        pe.wait_ge(a_vf, g * NC + (c + 1))
                        pe.wait_ge(a_k, g * NC + (c + 1))
                    wait(pe, a_ex, n - 1)
                    tok = slice(S * j, S * (j + 1))
                    for m in range(2):
                        sc = quads(A_S[u % 2][:, m, :])
                        pe.matmul(sc, idb[:, :], maskb[:, :].unsqueeze(1).broadcast_to([128, HG, S]),
                                  start=True, stop=False, skip_group_check=True)
                        for h in range(HG):
                            last = pe.matmul(sc[:, h, :], qab[:, c % 2, m, h, tok], kva[:, c % 2, m, tok],
                                             start=False, stop=h == HG - 1, skip_group_check=True)
                    last.then_inc(a_sc, 1)
                two = not (first and u < 2) and not (drain and u >= 2)
                if two:
                    pe.wait_ge(a_dn, n - 1)
                    wait(pe, a_pt, n - 2)
                    if first and u == 2:
                        pe.wait_ge(ln_h, 2 * 2 + KT)
                    for h in range(HG):
                        last = pe.transpose(quads(bank(PTB))[:, h, :], ea[:, u % 2, 0, h, :], idf[:, :])
                    last.then_inc(a_tp, 1)
                slot(1)
                if two:
                    w = (u - 2) % UN
                    pe.wait_ge(a_pt, n - 1)
                    wait(pe, a_ol, n - 2)
                    pe.matmul(bank(OB), quads(kva[:, (w // CB) % 2, 2, :])[:, w % CB, :],
                              pt[:, u % 2, :, :], start=True, stop=True).then_inc(a_pv, 1)
                if not (first and u < 3):
                    if u == 3:
                        pe.wait_ge(a_wol, g + 1)
                    pe.wait_ge(a_ol, n - 2)
                    wait(pe, a_y, n - 3)
                    for h in range(HG):
                        for i, (o_, w_) in enumerate(((oah, woh), (oah, wol), (oal, woh))):
                            last = pe.matmul(ps[:, YB, 0:DM], o_[:, (u - 3) % 2, h, :], w_[:, h, :],
                                             start=h == 0 and i == 0, stop=h == HG - 1 and i == 2)
                    last.then_inc(a_wo, 1)
                slot(2)

            def b_prep(g_to, t, bk):
                pe.wait_ge(b_raw_s, g_to * 16 + 16)
                p, k = t // 3, t % 3
                cols = {0: [(2 * p, 0, 128)], 1: [(2 * p, 128, 64), (2 * p + 1, 0, 64)],
                        2: [(2 * p + 1, 64, 128)]}[k]
                for kt in range(KT):
                    at = 128 * kt
                    for h, a, w in cols:
                        pe.matmul(bk[:, at:at + w],
                                  raw_b[:, RB_WQ + h * DM + 128 * kt:RB_WQ + h * DM + 128 * (kt + 1)],
                                  raw_b[:, RB_KCQ + h * XQ + a:RB_KCQ + h * XQ + a + w], start=True, stop=True)
                        at += w
                for m in range(2):
                    a = RB_QR + (2 * p + m) * 2 * XQ + 128 * k
                    last = pe.matmul(bk[:, 256 + 128 * m:384 + 128 * m], raw_b[:, a:a + 128],
                                     raw_b[:, RB_KR + 128 * p:RB_KR + 128 * (p + 1)], start=True, stop=True)
                return last

            def b_do(g_to, c, what, n):
                kind, t = what
                if kind == "qr":
                    q = (g_to * NC + c) * XP + t
                    pe.wait_ge(b_if, n + 1)
                    wait(pe, b_qs, q)
                    if isinstance(q, int) and q == XP:
                        pe.wait_ge(ln_h, 2 * 2 * NC)
                    t0, t1, t2 = 3 * t, 3 * t + 1, 3 * t + 2
                    o = bank(QRB)
                    for m in range(2):
                        pe.matmul(o, mq[:, t1, m, :], qcs[:, t1, m, :], start=m == 0, stop=False,
                                  skip_group_check=True)
                    for m in range(2):
                        pe.matmul(o[0:64, :], mq[:, t0, m, 0:64], qcs[:, t0, m, :], start=False, stop=m == 1,
                                  skip_group_check=True)
                        last = pe.matmul(o[64:128, :], mq[:, t2, m, 64:128], qcs[:, t2, m, :], start=False,
                                         stop=m == 1, skip_group_check=True)
                    last.then_inc(b_qr, 1)
                    return
                bk = bank(2 + n_par(n))
                wait(pe, b_if, n - 1)
                if kind == "prep":
                    b_prep(g_to, t, bk).then_inc(b_it, 1)
                    return
                if kind == "qb":
                    if c == 0:
                        pe.wait_ge(b_if, prep_of(g_to, t) + 1)
                    last = three_pass(bk, lambda kt: wbh[:, t, kt, :], lambda kt: wbl[:, t, kt, :], c)
                else:
                    for i in range(2):
                        h = 2 * t + i
                        last = pe.matmul(bk[64 * i:64 * i + 64, 0:DM], raw_b[:, RB_KV + h * XC:RB_KV + (h + 1) * XC],
                                         raw_b[:, RB_WO + h * DM:RB_WO + (h + 1) * DM], start=True, stop=True)
                last.then_inc(b_it, 1)

            def n_par(n):
                return n % 2 if isinstance(n, int) else place[0] % 2
            place = [0]

            def prep_of(g_to, t):
                if isinstance(g_to, int) and g_to == 0:
                    return t
                slots = [k for k in B_PLACE if k[2] == ("prep", t)]
                return (g_to - 1) * BN + (BF + B_PLACE[slots[0]])

            def b_unit(g, u, first=False, final=False, drain=False):
                n, c, j = g * UN + u, u // CB, u % CB

                def slot(s):
                    for what in B_EXTRA.get((a_part(first, final, drain), u, s), []):
                        if what[0] == "ln":
                            if what[1:3] == (9, 1):
                                pe.wait_ge(ln_h, 2 * 8 + 1)
                            if what[1] == 8:
                                pe.wait_ge(b_if, BF + (NG - 1) * BN + len(B_PLACES[True]))
                            if what[1:3] == (9, 0):
                                pe.wait_ge(b_qs, XP * NG * NC)
                            if drain:
                                pe.wait_ge(ln_h, 2 * 9 + 2)
                                pe.wait_ge(c_gs, 1)
                            ln_turn(*what[1:])
                        elif what[0] == "logits":
                            c_logits(*what[1:])
                        else:
                            c_turn(*what[1:])
                    if drain:
                        return
                    if first and s == 1 and u < KT:
                        if u:
                            pe.wait_ge(ln_h, 2 * (2 * NC - 1) + 1)
                        ln_turn(2 * NC - 1, u, QRB)
                    if first and c < NC - 1 and (u % CB, s) == (0, 0):
                        ln_ready(NC + c + 1)
                    for what in b_slot(u, s, final):
                        ahead = c == NC - 1 or what[0] == "prep"
                        g_to = g + 1 if ahead and what[0] != "wco" else g
                        if what[0] == "qr":
                            item = b_last(g, u, s, "qb", 3 * what[1] + 2)
                        else:
                            item = b_item(g, u, s, what)
                            place[0] = b_places(g)[u, s, what]
                        b_do(g_to, (c + 1) % NC, what, item)
                slot(0)
                if not drain:
                    if j == 0:
                        pe.wait_ge(b_qs, (g * NC + (c + 1)) * XP)
                    wait(pe, b_ex, n - 1)
                    for p in range(XP):
                        last = pe.matmul(B_S[u % 2][:, 256 * p:256 * (p + 1)],
                                         qr[:, c % 2, p, S * j:S * (j + 1)], kbd[:, u, :, :], start=True, stop=True)
                    last.then_inc(b_sc, 1)
                two = not (first and u < 2) and not (drain and u >= 2)
                if two:
                    pe.wait_ge(b_dn, n - 1)
                    wait(pe, b_pt, n - 2)
                    for h in range(HG):
                        last = pe.transpose(quads(bank(PTB))[:, h, :], eb[:, u % 2, h, :], idf[:, :])
                    last.then_inc(b_tp, 1)
                slot(1)
                if two:
                    w = (u - 2) % UN
                    pe.wait_ge(b_pt, n - 1)
                    wait(pe, b_ol, n - 2)
                    for i in range(2):
                        last = pe.matmul(ps[64 * i:64 * i + 64, OB, 0:XP * S], kvr[:, w, 0, :],
                                         pt[:, u % 2, i:HG:2, :], start=True, stop=True)
                    last.then_inc(b_pv, 1)
                if not (first and u < 3):
                    if u == 3:
                        pe.wait_ge(b_if, b_item(g, 2, 2, ("wco", 1)) + 1)
                    pe.wait_ge(b_ol, n - 2)
                    wait(pe, b_y, n - 3)
                    for p in range(XP):
                        for i, (o_, w_) in enumerate(((obh, wcoh), (obh, wcol), (obl, wcoh))):
                            last = pe.matmul(ps[:, YB, 0:DM], o_[:, (u - 3) % 2, p, :], w_[:, p, :],
                                             start=p == 0 and i == 0, stop=p == XP - 1 and i == 2)
                    last.then_inc(b_wo, 1)
                slot(2)

            def c_logits(p, bk):
                pe.wait_ge(c_gws, 16)
                pe.wait_ge(ln_f, (2 * NC + (p + 1) * NC // GP) * KT)
                if p == 0:
                    pe.wait_ge(ln_h, 2 * 8 + 2)
                for i in range(GB):
                    b = GB * p + i
                    for kt in range(KT):
                        last = pe.matmul(ps[:, bk, E * i:E * (i + 1)], xnf[:, kt, S * b:S * (b + 1)], gw[:, kt, :],
                                         start=kt == 0, stop=kt == KT - 1)
                last.then_inc(c_lg, 1)

            def c_turn(r, bk):
                pe.wait_ge(c_gs, (r // (NC // GP) + 1) * GATE_STEPS)
                tb = ps[0:KC, bk, :].bitcast(bf16)
                for j in range(CB):
                    last = pe.transpose(tb[:, S * j:S * (j + 1)], cmb[:, CB * r + j, :], idb[:, :])
                last.then_inc(c_ct, 1)

            pe.wait_ge(s_const, 16)
            for c in range(len(A_START)):
                for kt in range(KT):
                    ln_turn(c, kt, ln_bank(c, kt))
                if c == 0:
                    ln_ready(0)
                for item in A_START[c]:
                    if item == AV:
                        pe.wait_ge(a_wvl, 16)
                    a_project(0, 0, item, True, A_TURNS)
            pe.wait_ge(a_vf, 1)
            pe.wait_ge(s_cst, 2)
            pe.wait_ge(a_wld, 32)
            for u in range(UN):
                a_unit(0, u, first=True)
            with pe.Fori(1, NG - 1) as g:
                for u in range(UN):
                    a_unit(g, u)
            for u in range(UN):
                a_unit(NG - 1, u, final=True)
            for u in range(3):
                a_unit(NG, u, drain=True)

            pj_taken(held.pop())
            pe.wait_ge(b_kvc, NC)
            item = XT + 4
            for what in B_FIRST[item:]:
                b_do(0, 0, what, item - 1 if what[0] == "qr" else item)
                item += what[0] != "qr"
            pe.wait_ge(a_y, NG * UN)
            for u in range(UN):
                b_unit(0, u, first=True)
            with pe.Fori(1, NG - 1) as g:
                for u in range(UN):
                    b_unit(g, u)
            for u in range(UN):
                b_unit(NG - 1, u, final=True)
            for u in range(3):
                b_unit(NG, u, drain=True)

            pe.wait_ge(b_y, NG * UN)
            pe.wait_ge(c_cc, NC // GP)

            def c_down(v, g, c, t):
                pe.wait_ge(c_l, v + 1)
                if t == 0:
                    wait(pe, c_y, g * NC + c)
                par = (TG * c + t) % 2
                for j in range(CB):
                    for i, (h_, w_) in enumerate(((hhh, wch), (hhh, wcl), (hhl, wch))):
                        last = pe.matmul(ps[:, j // 2, DM * (j % 2):DM * (j % 2 + 1)],
                                         h_[:, par, S * j:S * (j + 1)], w_[:, t, 2 * KT * 128:RC_T],
                                         start=t == 0 and j % 2 == 0 and i == 0, stop=t == TG - 1 and i == 2,
                                         skip_group_check=True)
                last.then_inc(c_dn, 1)

            def c_unit(g, c, t, first=False):
                k = TG * c + t
                v = g * (NC * TG) + k
                if c == 0:
                    pe.wait_ge(c_lo, g * TG + (t + 1))
                tok = slice(CW * c, CW * (c + 1))
                if first and t == 0:
                    ln_ready(2 * NC + c)
                wait(pe, c_sg, v - 1)
                three_pass(bank(C_G[k % 2]), lambda kt: wch[:, t, 128 * kt:128 * (kt + 1)],
                           lambda kt: wcl[:, t, 128 * kt:128 * (kt + 1)], c).then_inc(c_g, 1)
                wait(pe, c_hu, v - 1)
                three_pass(bank(C_U[k % 2]), lambda kt: wch[:, t, 256 + 128 * kt:384 + 128 * kt],
                           lambda kt: wcl[:, t, 256 + 128 * kt:384 + 128 * kt], c).then_inc(c_u, 1)
                wait(pe, c_h, v - 1)
                if first and k == 2:
                    c_logits(1, C_C[0])
                    pe.wait_ge(c_gs, GATE_STEPS + 1)
                if first and k in (6, 8):
                    c_turn(k // 2 - 1, C_C[0])
                    pe.wait_ge(c_cc, k // 2)
                pe.matmul(bank(C_C[k % 2]), sel[:, t, :], combt[:, tok], start=True, stop=True).then_inc(c_c, 1)
                if first and k == 0:
                    for kt in range(KT):
                        ln_turn(3 * NC - 1, kt, kt)
                if first and k == 1:
                    pe.wait_ge(ln_h, 3 * NC * KT)
                if not (first and k == 0):
                    c_down(v - 1, g if k else g - 1, ((k - 1) // TG) % NC, (k - 1) % TG)

            for c in range(NC):
                for t in range(TG):
                    c_unit(0, c, t, first=True)
            with pe.Fori(1, CG) as g:
                for c in range(NC):
                    for t in range(TG):
                        c_unit(g, c, t)
            c_down(CG * NC * TG - 1, CG - 1, NC - 1, TG - 1)

        @block.vector
        def _(dve):
            def ln_stats(m):
                c = m % NC
                if m < NC:
                    dve.wait_ge(s_x[c], 16)
                else:
                    dve.wait_ge((a_y, b_y)[m // NC - 1], (NG - 1) * UN + CB * (c + 1))
                seqs = range(CB * c, CB * (c + 1))
                for b in seqs:
                    last = dve.bn_stats(stats[:, b, :], x_sb[:, b, :])
                last.then_inc(ln_st, 1)
                dve.wait_ge(ln_st, m + 1)
                for b in seqs:
                    last = dve.bn_aggr(mv[:, b, :], stats[:, b, :])
                last.then_inc(ln_ag, 1)
                dve.wait_ge(ln_ag, m + 1)
                dve.tensor_scalar(veps[:, CB * c:CB * (c + 1)], mv[:, CB * c:CB * (c + 1), 1], LN_EPS, None,
                                  ALU.add).then_inc(ln_var, 1)

            def ln_norm(m):
                c = m % NC
                dve.wait_ge(ln_rs, m + 1)
                wait(dve, ln_tp, 2 * (m - 2) + 2)
                for j in range(CB):
                    b = CB * c + j
                    last = dve.tensor_scalar(xnt[:, c % 2, j, :], x_sb[:, b, :], mv[:, b, 0:1], rstd[:, b:b + 1],
                                             ALU.subtract, ALU.mult)
                last.then_inc(ln_xt, 1)

            def ln_low(m):
                tok = slice(CW * (m % NC), CW * (m % NC + 1))
                dve.wait_ge(ln_h, 2 * m + 1)
                dve.tensor_tensor(xnl[:, 0, tok], xnf[:, 0, tok], xnh[:, 0, tok].bitcast(f32),
                                  ALU.subtract).then_inc(ln_l, 1)

            def layer_norm(stage):
                first = stage * NC
                for m in range(first, first + NC):
                    ln_stats(m)
                for m in range(first, first + NC):
                    ln_norm(m)
                    if m > first:
                        ln_low(m - 1)
                ln_low(first + NC - 1)

            def a_take(g_to, c, item, between=lambda: None, turns=1):
                chunk = g_to * NC + c
                if item == AV:
                    between()
                    return
                dve.wait_ge(a_pj, chunk * AN + (item + 1))
                src, par = quads(bank(PJ - (item % turns if turns > 1 else 0))), c % 2
                if item == 0:
                    to = ((kva[:, par, 0, :], 2), (kva[:, par, 1, :], 5))
                elif item == 1:
                    wait(dve, a_k, chunk)
                    to = ((ktmp[:, 0, :], 3), (ktmp[:, 1, :], 4))
                else:
                    h = a_tile(item) - 2
                    to = ((qab[:, par, 0, h, :], 0), (qab[:, par, 1, h, :], 1))
                for i, (dst, tab) in enumerate(to):
                    last = dve.tensor_tensor(quads(dst), src, bcast(taba[:, tab, :]), ALU.mult)
                    if i == 0:
                        between()
                last.then_inc(a_pf, 1)

            def kv_step(i):
                half = XC // 2
                if i == 0:
                    dve.wait_ge(b_ctx, 48)
                    for d in (0, half):
                        dve.tensor_tensor(kvt[:, :, d:d + half], kvin[:, :, half - d:XC - d],
                                          kvtab[:, 1, d:d + half].unsqueeze(1).broadcast_to([128, B, half]),
                                          ALU.mult).then_inc(b_kv, 1)
                elif i == 1:
                    dve.wait_ge(a_pv, NG * UN - CB)
                    dve.tensor_tensor(kvr[:, :, 0, :], kvin[:, :, :],
                                      kvtab[:, 0, :].unsqueeze(1).broadcast_to([128, B, XC]), ALU.mult).then_inc(b_kv, 1)
                else:
                    dve.wait_ge(b_kv, 3)
                    dve.tensor_tensor(kvr[:, :, 0, :], kvr[:, :, 0, :], kvt[:, :, :], ALU.add).then_inc(b_kv, 1)
                    dve.wait_ge(b_kv, 4)
                    dve.tensor_copy(kvr[:, :, 1, :], kvr[:, :, 0, :]).then_inc(b_kv, 1)

            def a_rec2(n, par):
                dve.wait_ge(a_ex, n + 1)
                dve.reciprocal(rec2[:, par, :], sums[:, par, 4:8]).then_inc(a_r2, 1)

            def a_ratio(n, par):
                dve.wait_ge(a_r2, n + 1)
                dve.tensor_tensor(ratio[:, par, :], rec2[:, par, :], sums[:, par, 0:4], ALU.mult).then_inc(a_rt, 1)

            def a_rho(n, par, g):
                dve.wait_ge(a_rt, n + 1)
                dve.tensor_tensor(rho[:, par, :], ratio[:, par, :], nlam[:, bass.ds(g * HG, HG)], ALU.mult)\
                   .then_inc(a_rh, 1)

            def a_diff(n, par):
                dve.wait_ge(a_rh, n + 1)
                for h in range(HG):
                    last = dve.scalar_tensor_tensor(out=ea[:, par, 0, h, :], in0=ea[:, par, 1, h, :],
                                                    scalar=rho[:, par, h:h + 1], in1=ea[:, par, 0, h, :],
                                                    op0=ALU.mult, op1=ALU.add)
                last.then_inc(a_df, 1)

            def a_den(n, par):
                dve.wait_ge(a_re, n + 1)
                dve.scalar_tensor_tensor(out=den[:, par, :], in0=sums[:, par, 0:4], scalar=DIFF_EPS,
                                         in1=rsum[:, par, :], op0=ALU.mult, op1=ALU.add).then_inc(a_dd, 1)

            def a_rden(n, par):
                dve.wait_ge(a_dd, n + 1)
                dve.reciprocal(rden[:, par, :], den[:, par, :]).then_inc(a_cb, 1)

            def add_x(b, done, n, added):
                dve.wait_ge(done, n + 1)
                dve.tensor_tensor(x_sb[:, b, :], ps[:, YB, 0:DM], x_sb[:, b, :], ALU.add).then_inc(added, 1)

            def a_unit(g, u, first=False, final=False, drain=False):
                n, c, j = g * UN + u, u // CB, u % CB
                one = not (first and u < 1) and not (drain and u >= 1)
                two = not (first and u < 2) and not (drain and u >= 2)

                def slot(s, between):
                    if not drain and (j, s) in A_SLOT and not (final and c == NC - 1):
                        a_take(g + 1 if c == NC - 1 else g, (c + 1) % NC, A_SLOT[j, s], between)
                    else:
                        between()
                    for what in A_EXTRA.get((a_part(first, final, drain), u, s), []):
                        if what[0] == "prep":
                            b_take(what, what[1], None, what[1], bank(PJ))
                        if what[0] == "qb":
                            b_take(what, BF // 2 + what[1], (BF // 2 + what[1]) % 2, None)
                if two:
                    a_den(n - 2, u % 2)
                if not (first and u < 4):
                    add_x((u - 4) % UN, a_wo, n - 4, a_y)
                if two:
                    a_rden(n - 2, u % 2)
                if one:
                    a_rec2(n - 1, (u - 1) % 2)
                slot(0, (lambda: a_ratio(n - 1, (u - 1) % 2)) if one else (lambda: None))
                if one:
                    a_rho(n - 1, (u - 1) % 2, g if u else g - 1)
                    a_diff(n - 1, (u - 1) % 2)
                if not (first and u < 3) and not (drain and u >= 3):
                    dve.wait_ge(a_o, n - 2)
                    wait(dve, a_wo, n - 4)
                    dve.tensor_tensor(oal[:, (u - 3) % 2, :, :], quads(bank(OB)),
                                      oah[:, (u - 3) % 2, :, :].bitcast(f32), ALU.subtract).then_inc(a_ol, 1)
                if not drain:
                    dve.wait_ge(a_sc, n + 1)
                    wait(dve, a_ex, n - 1)
                    dve.tensor_reduce(negmax[:, u % 2, :], A_S[u % 2].rearrange("p m (h k) -> p (m h) k", k=S),
                                      axis=AX.X, op=ALU.max, negate=True).then_inc(a_mx, 1)
                if u == 3 and not drain:
                    dve.wait_ge(a_woh, g + 1)
                    dve.tensor_tensor(wol[:, :, :], wo[:, bass.ds(g * HG, HG), :], woh[:, :, :].bitcast(f32),
                                      ALU.subtract).then_inc(a_wol, 1)
                slot(1, lambda: None)
                if first and u == 0:
                    ln_norm(2)
                    ln_stats(3)
                if first and u == 1:
                    ln_norm(3)
                if first and u == 2:
                    ln_low(2)
                if first and u == 7:
                    ln_low(3)
                if final and u == 8:
                    ln_stats(4)
                if final and u == 10:
                    ln_norm(4)
                if final and u == 12:
                    ln_low(4)
                    ln_stats(5)
                    kv_step(0)
                if final and u == 13:
                    ln_norm(5)
                    kv_step(1)
                if final and u == 14:
                    kv_step(2)
                if final and u == 15:
                    ln_stats(6)
                    ln_low(5)
                if drain and u == 0:
                    ln_norm(6)
                if drain and u == 2:
                    ln_low(6)
                slot(2, lambda: None)

            def b_take(what, n, par, m_done, bk=None, w_done=None):
                kind, t = what
                if kind == "qr":
                    return
                if bk is None:
                    bk = bank(2 + par)
                dve.wait_ge(b_it, n + 1)
                if kind == "qb":
                    for m in range(2):
                        last = dve.tensor_tensor(quads(qcs[:, t, m, :]), quads(bk), bcast(tabb[:, t % 3, m, :]),
                                                 ALU.mult)
                elif kind == "prep":
                    dve.wait_ge(b_m, m_done + 1)
                    last = dve.tensor_tensor(wbl[:, t, :, :].rearrange("p k n -> p (k n)"), bk[:, 0:256],
                                             wbh[:, t, :, :].rearrange("p k n -> p (k n)").bitcast(f32), ALU.subtract)
                else:
                    dve.wait_ge(b_wh, w_done + 1)
                    last = dve.tensor_tensor(wcol[:, t, :], bk[:, 0:DM], wcoh[:, t, :].bitcast(f32), ALU.subtract)
                last.then_inc(b_if, 1)

            def b_unit(g, u, first=False, final=False, drain=False):
                n = g * UN + u

                def slot(s):
                    if drain:
                        return
                    for what in b_slot(u, s, final):
                        if what[0] != "qr":
                            b_take(what, b_item(g, u, s, what), b_places(g)[u, s, what] % 2, (g + 1) * XT + what[1],
                                   w_done=g * XP + what[1])
                slot(0)
                if not (first and u < 3) and not (drain and u >= 3):
                    dve.wait_ge(b_o, n - 2)
                    wait(dve, b_wo, n - 4)
                    dve.tensor_tensor(obl[:, (u - 3) % 2, :, :].rearrange("p k n -> p (k n)"), ps[:, OB, 0:XP * S],
                                      obh[:, (u - 3) % 2, :, :].rearrange("p k n -> p (k n)").bitcast(f32),
                                      ALU.subtract).then_inc(b_ol, 1)
                if not drain:
                    dve.wait_ge(b_sc, n + 1)
                    wait(dve, b_ex, n - 1)
                    dve.tensor_reduce(negmax[:, u % 2, 0:HG], quads(B_S[u % 2]), axis=AX.X, op=ALU.max,
                                      negate=True).then_inc(b_mx, 1)
                if not (first and u < 1) and not (drain and u >= 1):
                    par = (u - 1) % 2
                    dve.wait_ge(b_ex, n)
                    wait(dve, b_dn, n - 2)
                    dve.reciprocal(rsum[:, par, :], sums[:, par, 0:HG]).then_inc(b_rs, 1)
                slot(1)
                if not (first and u < 3):
                    add_x((u - 3) % UN, b_wo, n - 3, b_y)
                slot(2)
                if first and u == 2:
                    ln_low(2 * NC - 1)
                if final and u == 7:
                    ln_stats(8)
                if final and u == 8:
                    ln_norm(8)
                if final and u == 10:
                    ln_stats(9)
                if final and u == 11:
                    ln_norm(9)
                if final and u == 12:
                    ln_low(8)
                    c_zero()
                if final and u == 13:
                    gate_take(0, 3)
                    gate(0, 0)
                    ln_low(9)
                if final and u == 14:
                    gate(0, 1)
                    gate(0, 2)
                if final and u == 15:
                    ln_stats(10)
                    gate(0, 3)
                if drain and u == 0:
                    ln_norm(10)
                    gate(0, 4)
                if drain and u == 1:
                    ln_low(10)
                if drain and u == 2:
                    ln_stats(11)

            steps = [0]

            def step(ins):
                steps[0] += 1
                ins.then_inc(c_gs, 1)
                dve.wait_ge(c_gs, steps[0])

            def c_zero():
                dve.wait_ge(b_qr, XP * NG * NC)
                dve.memset(cmb[:, :, :], 0.0).then_inc(c_z, 1)
                dve.memset(gone[:, :, :], 1.0).then_inc(c_z, 1)
                dve.wait_ge(c_z, 2)
                dve.memset(cmb[:, :, 3 * E:3 * E + 1], 1.0)
                dve.memset(gone[:, :, 0:1], 0.0)

            def gate_take(p, bk):
                dve.wait_ge(c_lg, p + 1)
                step(dve.tensor_copy(gl[:, GB * p:GB * (p + 1), :],
                                     ps[:, bk, 0:GB * E].rearrange("p (b e) -> p b e", e=E)))

            def gate(p, i):
                bs = slice(GB * p, GB * (p + 1))
                flat = "p b e -> p (b e)"

                def over_e(ap):
                    return ap.unsqueeze(2).broadcast_to([128, GB, E])
                thr = g8[:, bs, TOPK - 1:TOPK].broadcast_to([128, GB, E])
                if i == 0:
                    step(dve.tensor_reduce(gmx[:, bs], gl[:, bs, :], axis=AX.X, op=ALU.max, negate=True))
                    step(dve.tensor_tensor(gl[:, bs, :], gl[:, bs, :], over_e(gmx[:, bs]), ALU.add))
                elif i == 1:
                    dve.wait_ge(c_ge, p + 1)
                    step(dve.tensor_reduce(gsum[:, bs], ge[:, bs, :], axis=AX.X, op=ALU.add))
                    step(dve.reciprocal(grec[:, bs], gsum[:, bs]))
                    step(dve.tensor_tensor(gp[:, bs, :], ge[:, bs, :], over_e(grec[:, bs]), ALU.mult))
                    for b in range(GB * p, GB * (p + 1)):
                        last = dve.max(g8[:, b, :], gp[:, b, :])
                    step(last)
                elif i == 2:
                    step(dve.tensor_tensor(ggt[:, bs, :], gp[:, bs, :], thr, ALU.is_gt))
                    step(dve.tensor_tensor(geq[:, bs, :], gp[:, bs, :], thr, ALU.is_equal))
                    step(dve.tensor_reduce(gn[:, bs], ggt[:, bs, :], axis=AX.X, op=ALU.add))
                    step(dve.tensor_scalar(glim[:, bs], gn[:, bs], -1.0, float(TOPK), ALU.mult, ALU.add))
                    step(dve.tensor_tensor_scan(gcum[:, bs, :].rearrange(flat), gone[:, bs, :].rearrange(flat),
                                                geq[:, bs, :].rearrange(flat), 0.0, ALU.mult, ALU.add))
                elif i == 3:
                    step(dve.tensor_tensor(gcum[:, bs, :], gcum[:, bs, :], over_e(glim[:, bs]), ALU.is_le))
                    step(dve.tensor_tensor(gcum[:, bs, :], gcum[:, bs, :], geq[:, bs, :], ALU.mult))
                    step(dve.tensor_tensor(gcum[:, bs, :], gcum[:, bs, :], ggt[:, bs, :], ALU.add))
                    step(dve.tensor_tensor(gp[:, bs, :], gp[:, bs, :], gcum[:, bs, :], ALU.mult))
                else:
                    step(dve.tensor_copy(cmb[:, bs, 0:E], gp[:, bs, :]))
                    step(dve.tensor_tensor(gr1[:, bs, :], gp[:, bs, :], cmb[:, bs, 0:E], ALU.subtract))
                    step(dve.tensor_copy(cmb[:, bs, E:2 * E], gr1[:, bs, :]))
                    step(dve.tensor_tensor(gr2[:, bs, :], gr1[:, bs, :], cmb[:, bs, E:2 * E], ALU.subtract))
                    step(dve.tensor_copy(cmb[:, bs, 2 * E:3 * E], gr2[:, bs, :]))
                    assert steps[0] == (p + 1) * GATE_STEPS

            ln_stats(0)
            ln_norm(0)
            ln_stats(1)
            ln_low(0)
            dve.wait_ge(a_tab, 16)
            ln_norm(1)
            dve.wait_ge(s_const, 16)
            dve.wait_ge(s_mask, 16)
            dve.tensor_copy(idb[:, :], idf[:, :]).then_inc(s_cst, 1)
            dve.tensor_copy(maskb[:, :], maskf[:, :]).then_inc(s_cst, 1)
            for item in A_START[0]:
                a_take(0, 0, item, turns=A_TURNS)
            ln_low(1)
            for item in A_START[1]:
                a_take(0, 0, item, turns=A_TURNS)
            ln_stats(2)
            dve.wait_ge(a_wld, 32)
            dve.tensor_scalar(nlam[:, :], nlam[:, :], -1.0, None, ALU.mult).then_inc(a_nl, 1)
            dve.wait_ge(a_nl, 1)
            for u in range(UN):
                a_unit(0, u, first=True)
            with dve.Fori(1, NG - 1) as g:
                for u in range(UN):
                    a_unit(g, u)
            for u in range(UN):
                a_unit(NG - 1, u, final=True)
            for u in range(4):
                a_unit(NG, u, drain=True)

            ln_stats(2 * NC - 1)
            dve.wait_ge(a_wo, NG * UN)
            item = XT + 4
            for what in B_FIRST[item:]:
                b_take(what, item, item % 2, what[1])
                item += what[0] != "qr"
            ln_norm(2 * NC - 1)
            for u in range(UN):
                b_unit(0, u, first=True)
            with dve.Fori(1, NG - 1) as g:
                for u in range(UN):
                    b_unit(g, u)
            for u in range(UN):
                b_unit(NG - 1, u, final=True)
            for u in range(3):
                b_unit(NG, u, drain=True)

            def c_add(v, c, added):
                dve.wait_ge(c_dn, v + 1)
                for i in range(2):
                    dst = x_sb[:, CB * c + 2 * i:CB * c + 2 * i + 2, :].rearrange("p b d -> p (b d)")
                    last = dve.tensor_tensor(dst, bank(i), dst, ALU.add)
                last.then_inc(c_y, 1)

            def c_unit(g, c, t, first=False):
                k = TG * c + t
                v, par = g * (NC * TG) + k, k % 2
                dve.wait_ge(c_u, v + 1)
                dve.wait_ge(c_sg, v + 1)
                dve.tensor_tensor(hu[:, par, :], bank(C_U[par]), sg[:, par, :], ALU.mult).then_inc(c_hu, 1)
                dve.wait_ge(c_hu, v + 1)
                if first and k == 2:
                    gate_take(1, C_C[0])
                dve.wait_ge(c_c, v + 1)
                dve.tensor_tensor(hh[:, par, :], bank(C_C[par]), hu[:, par, :], ALU.mult).then_inc(c_h, 1)
                dve.wait_ge(c_hr, v + 1)
                dve.tensor_tensor(hhl[:, par, :], hh[:, par, :], hhh[:, par, :].bitcast(f32), ALU.subtract)\
                   .then_inc(c_l, 1)
                if t == 0 and not (first and k == 0):
                    c_add(v - 1, (c - 1) % NC, None)
                if first and k == 1:
                    ln_low(3 * NC - 1)
                if first and k == 2:
                    gate(1, 0)
                if first and k == 3:
                    gate(1, 1)
                if first and k == 4:
                    gate(1, 2)
                if first and k == 5:
                    gate(1, 3)
                    gate(1, 4)

            ln_norm(3 * NC - 1)
            for c in range(NC):
                for t in range(TG):
                    c_unit(0, c, t, first=True)
            with dve.Fori(1, CG) as g:
                for c in range(NC):
                    for t in range(TG):
                        c_unit(g, c, t)
            c_add(CG * NC * TG - 1, NC - 1, None)

        @block.scalar
        def _(act):
            def copy(dst, src):
                return act.activation(dst, src, ACT.Copy)

            def ln_take(m, kt, bk):
                tok = slice(CW * (m % NC), CW * (m % NC + 1))
                act.wait_ge(ln_tp, 2 * m + kt + 1)
                copy(xnf[:, kt, tok], bank(bk)).then_inc(ln_f, 1)
                copy(xnh[:, kt, tok], bank(bk)).then_inc(ln_h, 1)

            def layer_norm(stage):
                for c in range(NC):
                    for kt in range(KT):
                        ln_take(stage * NC + c, kt, ln_bank(c, kt))

            def a_high(g_to, tile):
                act.wait_ge(a_raw, g_to * 16 + 16)
                t = slice(128 * tile, 128 * (tile + 1))
                copy(wah[:, :, t], raw_a[:, :, t]).then_inc(a_hi, 1)

            def a_take_v(g_to, c, turns=1):
                act.wait_ge(a_pj, (g_to * NC + c) * AN + (AV + 1))
                copy(quads(kva[:, c % 2, 2, :]), quads(bank(PJ - AV % turns))).then_inc(a_vf, 1)

            def exps(n, u, maps, mx, ex, free, dst):
                par = u % 2
                act.wait_ge(mx, n + 1)
                wait(act, free, n - 1)
                for m in range(maps):
                    for h in range(HG):
                        i = m * HG + h
                        src = (A_S[par][:, m, :] if maps == 2 else B_S[par])
                        last = act.activation(dst(m, h), quads(src)[:, h, :], ACT.Exp, bias=negmax[:, par, i:i + 1],
                                              accum_out=sums[:, par, i:i + 1])
                last.then_inc(ex, 1)

            def a_unit(g, u, first=False, final=False, drain=False):
                n, c, j = g * UN + u, u // CB, u % CB

                def slot(s):
                    for what in A_EXTRA.get((a_part(first, final, drain), u, s), []):
                        if what[0] == "ln":
                            ln_take(what[1], what[2], PJ)
                        elif what[0] == "prep":
                            b_take(0, 0, what, what[1], None, bank(PJ))
                        elif what[0] == "kbd":
                            r = what[1]
                            act.wait_ge(b_kvp, r + 1)
                            if r == 0:
                                act.wait_ge(b_kz, 1)
                            for i in range(2):
                                rows = slice(64 * i, 64 * i + 64)
                                last = copy(kbd[rows, CB * r:CB * (r + 1), i, :], quads(bank(PJ))[rows])
                            last.then_inc(b_kvc, 1)
                    if drain or (j, s) not in A_SLOT or (final and c >= NC - 2 and not (c == NC - 2 and A_SLOT[j, s] == AV)):
                        return
                    item = A_SLOT[j, s]
                    if item == AV:
                        a_take_v(g + 1 if c == NC - 1 else g, (c + 1) % NC)
                    elif c == NC - 2:
                        act.wait_ge(a_pj, (g * NC + (NC - 1)) * AN + (item + 1))
                        a_high(g + 1, a_tile(item))
                slot(0)
                two = not (first and u < 2) and not (drain and u >= 2)
                if two:
                    act.wait_ge(a_tp, n - 1)
                    wait(act, a_pv, n - 3)
                    copy(pt[:, u % 2, :, :], quads(bank(PTB))).then_inc(a_pt, 1)
                if u == 3 and not drain:
                    if first:
                        act.wait_ge(a_wld, 32)
                    wait(act, a_wo, n - 3)
                    copy(woh[:, :, :], wo[:, bass.ds(g * HG, HG), :]).then_inc(a_woh, 1)
                if not (first and u < 1) and not (drain and u >= 1):
                    act.wait_ge(a_df, n)
                    par = (u - 1) % 2
                    wait(act, a_dd, n - 2)
                    for h in range(HG):
                        last = act.activation(ea[:, par, 0, h, :], ea[:, par, 0, h, :], ACT.Relu,
                                              accum_out=rsum[:, par, h:h + 1])
                    last.then_inc(a_re, 1)
                if not drain:
                    exps(n, u, 2, a_mx, a_ex, a_tp, lambda m, h: ea[:, u % 2, m, h, :])
                slot(1)
                if two:
                    act.wait_ge(a_pv, n - 1)
                    wait(act, a_wo, n - 3)
                    copy(oah[:, (u - 2) % 2, :, :], quads(bank(OB))).then_inc(a_o, 1)
                if first and u == 1:
                    for kt in range(KT):
                        ln_take(2, kt, PTB + kt)
                slot(2)

            def b_take(g_to, c, what, n, par, bk=None):
                kind, t = what
                if kind == "qr":
                    act.wait_ge(b_qr, (g_to * NC + c) * XP + (t + 1))
                    copy(qr[:, c % 2, t, :], bank(QRB)).then_inc(b_qs, 1)
                elif kind == "prep":
                    act.wait_ge(b_it, n + 1)
                    if bk is None:
                        bk = bank(2 + par)
                    copy(wbh[:, t, :, :].rearrange("p k n -> p (k n)"), bk[:, 0:256])
                    copy(mq[:, t, :, :].rearrange("p k n -> p (k n)"), bk[:, 256:512]).then_inc(b_m, 1)

                elif kind == "wco":
                    act.wait_ge(b_it, n + 1)
                    copy(wcoh[:, t, :], bank(2 + par)[:, 0:DM]).then_inc(b_wh, 1)

            def b_unit(g, u, first=False, final=False, drain=False):
                n, c = g * UN + u, u // CB

                def slot(s):
                    for what in B_EXTRA.get((a_part(first, final, drain), u, s), []):
                        if what[0] == "ln":
                            ln_take(*what[1:])
                        elif what[0] == "comb":
                            c_take_comb(*what[1:])
                    if final and s == 2 and u >= UN - CB:
                        c_high(0, u - (UN - CB))
                    if final and (u, s) == (UN - 1, 2):
                        c_high(0, TG - 1)
                    if final and (u, s) == (UN - 2, 1):
                        gate_exp(0)
                    if drain:
                        return
                    for what in b_slot(u, s, final):
                        if what[0] != "qb":
                            item = None if what[0] == "qr" else b_item(g, u, s, what)
                            par = None if item is None else b_places(g)[u, s, what] % 2
                            b_take(g + 1 if c == NC - 1 else g, (c + 1) % NC, what, item, par)
                slot(0)
                two = not (first and u < 2) and not (drain and u >= 2)
                if two:
                    act.wait_ge(b_tp, n - 1)
                    wait(act, b_pv, n - 3)
                    copy(pt[:, u % 2, :, :], quads(bank(PTB))).then_inc(b_pt, 1)
                if not drain:
                    exps(n, u, 1, b_mx, b_ex, b_tp, lambda m, h: eb[:, u % 2, h, :])
                slot(1)
                if two:
                    act.wait_ge(b_pv, n - 1)
                    wait(act, b_wo, n - 3)
                    copy(obh[:, (u - 2) % 2, :, :].rearrange("p k n -> p (k n)"), ps[:, OB, 0:XP * S]).then_inc(b_o, 1)
                slot(2)
                if first and u < KT:
                    ln_take(2 * NC - 1, u, QRB)

            def c_high(g_to, t):
                act.wait_ge(c_raw_s, g_to * 16 + 16)
                s0 = TG * RC_T + 128 * t
                copy(sel[:, t, :], raw_c[0:KC, s0:s0 + 128])
                copy(wch[:, t, :], raw_c[:, RC_T * t:RC_T * (t + 1)]).then_inc(c_hi, 1)

            def gate_exp(p):
                bs = slice(GB * p, GB * (p + 1))
                act.wait_ge(c_gs, p * GATE_STEPS + 3)
                act.activation(ge[:, bs, :], gl[:, bs, :], ACT.Exp).then_inc(c_ge, 1)

            def c_take_comb(r, bk):
                act.wait_ge(c_ct, r + 1)
                copy(combt[:, CW * r:CW * (r + 1)], ps[0:KC, bk, :].bitcast(bf16)[:, 0:CW]).then_inc(c_cc, 1)

            for tile in range(2):
                a_high(0, tile)
            for c in range(len(A_START)):
                for kt in range(KT):
                    ln_take(c, kt, ln_bank(c, kt))
                if c == 0:
                    for tile in range(2, AW):
                        a_high(0, tile)
            a_take_v(0, 0, A_TURNS)
            for u in range(UN):
                a_unit(0, u, first=True)
            with act.Fori(1, NG - 1) as g:
                for u in range(UN):
                    a_unit(g, u)
            for u in range(UN):
                a_unit(NG - 1, u, final=True)
            for u in range(3):
                a_unit(NG, u, drain=True)

            act.wait_ge(a_wo, NG * UN)
            for what in B_STEP:
                b_take(0, 0, what, None, None)
            act.wait_ge(a_dn, NG * UN)
            for u in range(UN):
                b_unit(0, u, first=True)
            with act.Fori(1, NG - 1) as g:
                for u in range(UN):
                    b_unit(g, u)
            for u in range(UN):
                b_unit(NG - 1, u, final=True)
            for u in range(3):
                b_unit(NG, u, drain=True)

            def c_unit(g, c, t, first=False):
                k = TG * c + t
                v, par = g * (NC * TG) + k, k % 2
                act.wait_ge(c_g, v + 1)
                wait(act, c_hu, v - 1)
                act.activation(sg[:, par, :], bank(C_G[par]), ACT.Silu).then_inc(c_sg, 1)
                if first and k in (6, 8):
                    c_take_comb(k // 2 - 1, C_C[0])
                act.wait_ge(c_h, v + 1)
                wait(act, c_dn, v - 1)
                copy(hhh[:, par, :], hh[:, par, :]).then_inc(c_hr, 1)
                if first and k == 0:
                    for kt in range(KT):
                        ln_take(3 * NC - 1, kt, kt)
                if first and k == 2:
                    gate_exp(1)
                if (c == NC - 1 and t >= 1) or (k == 0 and not first):
                    act.wait_ge(c_dn, v)
                    c_high(g if k == 0 else g + 1, (t - 1) % TG)

            for c in range(NC):
                for t in range(TG):
                    c_unit(0, c, t, first=True)
            with act.Fori(1, CG) as g:
                for c in range(NC):
                    for t in range(TG):
                        c_unit(g, c, t)

        @block.gpsimd
        def _(pool):
            def ln_rstd(m):
                cs = slice(CB * (m % NC), CB * (m % NC + 1))
                pool.wait_ge(ln_var, m + 1)
                pool.tensor_tensor(rstd[:, cs], veps[:, cs], mhalf[:, cs], ALU.pow).then_inc(ln_rs, 1)

            def ln_low(m):
                tok = slice(CW * (m % NC), CW * (m % NC + 1))
                pool.wait_ge(ln_h, 2 * m + 2)
                pool.tensor_tensor(xnl[:, 1, tok], xnf[:, 1, tok], xnh[:, 1, tok].bitcast(f32),
                                   ALU.subtract).then_inc(ln_l2, 1)

            def layer_norm(stage):
                for m in range(stage * NC, (stage + 1) * NC):
                    ln_rstd(m)
                for m in range(stage * NC, (stage + 1) * NC):
                    ln_low(m)

            def a_low(g_to, tile):
                pool.wait_ge(a_hi, g_to * AW + (tile + 1))
                t = slice(128 * tile, 128 * (tile + 1))
                pool.tensor_tensor(wal[:, :, t], raw_a[:, :, t], wah[:, :, t].bitcast(f32), ALU.subtract)\
                    .then_inc(a_lo, 1)

            def a_keys(g_to, c):
                pool.wait_ge(a_pf, (g_to * NC + c) * AW + 2)
                for m in range(2):
                    last = pool.tensor_tensor(kva[:, c % 2, m, :], kva[:, c % 2, m, :], ktmp[:, m, :], ALU.add)
                last.then_inc(a_k, 1)

            def norm(n, par, ready, done, src, rec):
                pool.wait_ge(ready, n + 1)
                pool.tensor_tensor(src[:, par, :, :], src[:, par, :, :],
                                   rec[:, par, :].unsqueeze(2).broadcast_to([128, HG, S]), ALU.mult).then_inc(done, 1)

            def a_unit(g, u, first=False, final=False, drain=False):
                n, c, j = g * UN + u, u // CB, u % CB
                if not (first and u < 2):
                    norm(n - 2, u % 2, a_cb, a_dn, ea[:, :, 0, :, :], rden)
                if first and u == 2:
                    ln_low(2)
                if first and u == 7:
                    ln_low(3)
                if final and u == 8:
                    ln_rstd(4)
                if final and u == 12:
                    ln_low(4)
                    kbd_zero()
                if final and u == 13:
                    ln_rstd(5)
                if final and u == 15:
                    ln_low(5)
                if drain and u == 0:
                    ln_rstd(6)
                if drain:
                    return
                if final and c >= NC - 2:
                    if u == UN - 2 * CB:
                        a_keys(g, NC - 1)
                    return
                if j == 0:
                    a_keys(g + 1 if c == NC - 1 else g, (c + 1) % NC)
                if c == NC - 2:
                    for s in range(2):
                        if (j, s) in A_SLOT and A_SLOT[j, s] != AV:
                            a_low(g + 1, a_tile(A_SLOT[j, s]))

            def kbd_zero():
                pool.wait_ge(a_sc, NG * UN - CB)
                pool.memset(kbd[:, :, :, :], 0.0).then_inc(b_kz, 1)

            def c_low(g_to, t):
                pool.wait_ge(c_hi, g_to * TG + (t + 1))
                pool.tensor_tensor(wcl[:, t, :], raw_c[:, RC_T * t:RC_T * (t + 1)], wch[:, t, :].bitcast(f32),
                                   ALU.subtract).then_inc(c_lo, 1)

            pool.memset(mhalf[:, :], -0.5).then_inc(s_cst2, 1)
            pool.wait_ge(s_cst2, 1)
            ln_rstd(0)
            a_low(0, 0)
            a_low(0, 1)
            ln_rstd(1)
            ln_low(0)
            for tile in range(2, AW):
                a_low(0, tile)
            a_keys(0, 0)
            ln_low(1)
            ln_rstd(2)
            ln_rstd(3)
            for u in range(UN):
                a_unit(0, u, first=True)
            with pool.Fori(1, NG - 1) as g:
                for u in range(UN):
                    a_unit(g, u)
            for u in range(UN):
                a_unit(NG - 1, u, final=True)
            for u in range(2):
                a_unit(NG, u, drain=True)

            ln_low(2 * NC - 2)
            ln_rstd(2 * NC - 1)
            for u in range(1, UN):
                norm(u - 1, (u - 1) % 2, b_rs, b_dn, eb, rsum)
                if u == 2:
                    ln_low(2 * NC - 1)
            with pool.Fori(1, NG - 1) as g:
                for u in range(UN):
                    norm(g * UN + (u - 1), (u - 1) % 2, b_rs, b_dn, eb, rsum)
            for u in range(UN + 1):
                n = (NG - 1) * UN + u - 1
                norm(n, n % 2, b_rs, b_dn, eb, rsum)
                if u == 7:
                    ln_rstd(2 * NC)
                if u == 10:
                    ln_rstd(2 * NC + 1)
                if u in (12, 13):
                    ln_low(2 * NC + u - 12)
                if u in (14, 15):
                    c_low(0, u - 14)
                if u == 15:
                    ln_rstd(2 * NC + 2)
            for t in range(2, TG):
                c_low(0, t)

            ln_low(2 * NC + 2)
            ln_rstd(3 * NC - 1)
            ln_low(3 * NC - 1)
            with pool.Fori(1, CG) as g:
                for t in range(TG):
                    c_low(g, t)
            for t in range(TG - 1):
                c_low(CG, t)


_OUT = ((B, S, DM), "float32")


def _tables(np):
    f = np.float32
    pos = np.arange(S, dtype=f)

    def table(dim, rep):
        inv = (f(1.0) / np.power(f(10000.0), np.arange(0, dim, 2, dtype=f) / f(dim))).astype(f)
        ang = (pos[:, None] * inv[None, :]).astype(f).astype(np.float64)
        cos, sin = np.cos(ang), np.sin(ang)
        if rep:
            return np.repeat(cos, 2, axis=1), np.repeat(sin, 2, axis=1)
        return cos, sin
    c, s = (t.T for t in table(128, False))
    cc = lambda a, b: np.concatenate([a, b], axis=0)
    a_tab = np.stack([cc(c, s) / 8, cc(s, c) / 8, cc(c, -c), cc(-s, s), cc(c, c), cc(s, s)], axis=1)
    cq, sq = (t.T for t in table(XQ, True))
    half = XQ // 2
    sq = np.concatenate([sq[half:], -sq[:half]], axis=0)
    b_tab = np.stack([np.tile(cq, (2, 1)).reshape(3, 128, S), np.tile(sq, (2, 1)).reshape(3, 128, S)])
    b_tab = b_tab.transpose(2, 1, 0, 3)
    ck, sk = table(XC, True)
    sk = np.concatenate([-sk[:, :XC // 2], sk[:, XC // 2:]], axis=1)
    kv = np.stack([ck, sk], axis=1)
    q, k = np.arange(S)[:, None], np.arange(S)[None, :]
    mask = np.where((k <= q) & (k >= q - WINDOW + 1), 0.0, NEG)
    sel = np.zeros((CG + 1, 128, TG, 128))
    for g in range(CG + 1):
        for t in range(TG):
            for i in range(128):
                e = ((g % CG) * TG + t) * 128 + i
                rows = [e // EI + E * m for m in range(3)] if e < E * EI else [3 * E]
                sel[g, rows, t, i] = 1.0
    to = lambda a: np.ascontiguousarray(a.astype(f))
    return to(a_tab), to(b_tab), to(kv), to(mask), to(np.eye(128)), sel.astype(f)


def kernel(**inputs):
    import numpy as np
    import concourse.bacc as _bacc
    from concourse.bass_utils import run_bass_kernel_spmd as _run

    w = {k: np.asarray(v) for k, v in inputs.items()}
    a_tab, b_tab, kvtab, mask, ident, sel = _tables(np)
    f = np.float32

    def rows(a):
        return a.reshape(KT, 128, -1).transpose(1, 0, 2)

    def again(a):
        return np.concatenate([a, a[:1]], axis=0)
    wq, wk, wv = w["L0_attn_Wq"], w["L0_attn_Wk"], w["L0_attn_Wv"]
    a_wqk = []
    for g in range(NG):
        k = wk[:, 128 * g:128 * (g + 1)]
        a_wqk.append(rows(np.concatenate([k[:, :64], k[:, :64], k[:, 64:], k[:, 64:],
                                          wq[:, 512 * g:512 * (g + 1)]], axis=1)))
    a_wv = rows(wv)
    a_wo = w["L0_attn_Wo"].reshape(H, 128, DM).transpose(1, 0, 2)
    a_lam = np.broadcast_to(w["L0_attn_lam"][None, :], (128, H))

    xq = w["L0_xattn_Wq"].reshape(H, 128, DM)
    kcq, kckv = w["L0_xattn_w_kc_q"], w["L0_xattn_w_kc_kv"]
    wqr, wkr = w["L0_xattn_W_qr"], w["L0_xattn_W_kr"]
    xwo = w["L0_xattn_Wo"].T.reshape(H, 128, DM)
    b_raw = np.zeros((NG, 128, RB_N), f)
    for g in range(NG):
        for i in range(HG):
            h, p = HG * g + i, i // 2
            half = slice(64 * (i % 2), 64 * (i % 2) + 64)
            b_raw[g, :, RB_WQ + i * DM:RB_WQ + (i + 1) * DM] = xq[h]
            b_raw[g, :, RB_KCQ + i * XQ:RB_KCQ + (i + 1) * XQ] = kcq[h]
            b_raw[g, :, RB_KV + i * XC:RB_KV + (i + 1) * XC] = kckv[h]
            b_raw[g, :, RB_WO + i * DM:RB_WO + (i + 1) * DM] = xwo[h]
            b_raw[g, half, RB_KR + 128 * p + 64 * (i % 2):RB_KR + 128 * p + 64 * (i % 2) + 64] = wkr[h].T
            for m, rolled in enumerate((wqr[h], np.roll(wqr[h], -(XQ // 2), axis=0))):
                a = RB_QR + (2 * p + m) * 2 * XQ + XQ * (i % 2)
                b_raw[g, half, a:a + XQ] = rolled.T

    def hidden(moe, shared, r0, r1, s0, s1):
        a = np.zeros((IT * 128, DM), f)
        a[:E * EI] = moe[:, r0:r1].reshape(E * EI, DM)
        a[E * EI:E * EI + SI] = shared[s0:s1]
        return a
    w1, s1 = w["L0_ffn_w1"], w["L0_ffn_shared_w1"]
    gu = np.stack([hidden(w1, s1, 0, EI, 0, SI), hidden(w1, s1, EI, 2 * EI, SI, 2 * SI)])
    gu = gu.reshape(2, CG, TG, 128, KT, 128).transpose(1, 5, 2, 0, 4, 3).reshape(CG, 128, TG, 2 * KT * 128)
    dn = hidden(w["L0_ffn_w2"].transpose(0, 2, 1), w["L0_ffn_shared_w2"].T, 0, EI, 0, SI)
    dn = dn.reshape(CG, TG, 128, DM).transpose(0, 2, 1, 3)
    c_raw = again(np.concatenate([gu, dn], axis=3).reshape(CG, 128, TG * RC_T))
    c_raw = np.concatenate([c_raw, sel.reshape(CG + 1, 128, TG * 128)], axis=2)
    c_gate = rows(w["L0_ffn_gate_w"].T)

    nc = _bacc.Bacc("TRN2", target_bir_lowering=False, num_devices=1)
    given = dict(x=w["x"], ctx_in=w["ctx_512"], in_wqk=np.stack(a_wqk), in_wv=a_wv, in_wo=a_wo,
                 in_lam=a_lam, in_taba=a_tab, in_rawb=b_raw, in_tabb=b_tab, in_kvtab=kvtab, in_rawc=c_raw,
                 in_gate=c_gate, ident=ident, mask=mask)
    arrays, args = {}, {}
    for name, a in given.items():
        a = np.ascontiguousarray(a)
        arrays[f"{name}_dram"] = a
        args[name] = nc.dram_tensor(f"{name}_dram", a.shape, mybir.dt.from_np(a.dtype), kind="ExternalInput").ap()
    shape, dtype = _OUT
    args["out"] = nc.dram_tensor("out_0", shape, mybir.dt.from_np(np.dtype(dtype)), kind="ExternalOutput").ap()
    decoder_kernel(nc, **args)
    r = _run(nc, [arrays], core_ids=[0])
    return r.results[0]["out_0"]
```
